# Optimizing a Trainium2 kernel written in Bass

```python
import numpy as np
import jax
import jax.numpy as jnp

def _softmax(x, axis=-1):
    return jax.nn.softmax(x, axis=axis)

def _gelu(x):
    return jax.nn.gelu(x, approximate=True)

def _silu(x):
    return jax.nn.silu(x)

def _sigmoid(x):
    return jax.nn.sigmoid(x)

def _layernorm(x, axis=-1, eps=1e-05):
    m = jnp.mean(x, axis=axis, keepdims=True)
    v = jnp.var(x, axis=axis, keepdims=True)
    return (x - m) / jnp.sqrt(v + eps)

def _scatter_add(tgt, idx, src, axis=0):
    return tgt.at[idx].add(src)

def _segment_sum(src, seg, n):
    return jax.ops.segment_sum(src, seg, n)
kernel_name = 'mk_prb_d1_jaxref_r8_0b66a2'

def setup_inputs(seed: int=0):
    np.random.seed(seed)
    _w = jnp.asarray

    def _L0_attn_setup():
        import jax, jax.numpy as jnp
        import numpy as np
        D_MODEL = 128
        NHEAD = 16
        HEAD_DIM = D_MODEL // NHEAD
        MAX_POS = 256

        def _rope_tables(seq_len, dim):
            inv_freq = 1.0 / 10000.0 ** (jnp.arange(0, dim, 2, dtype=jnp.float32) / dim)
            t = jnp.arange(seq_len, dtype=jnp.float32)[:, None]
            freqs = t * inv_freq[None, :]
            emb = jnp.concatenate([freqs, freqs], axis=-1)
            return (jnp.cos(emb), jnp.sin(emb))

        def _rotate_half(x):
            x1, x2 = jnp.split(x, 2, axis=-1)
            return jnp.concatenate([-x2, x1], axis=-1)

        def _apply_rope(x, cos, sin):
            c = cos[None, :, None, :]
            s = sin[None, :, None, :]
            return x * c + _rotate_half(x) * s
        key = jax.random.key(seed)
        ks = jax.random.split(key, 9)
        B, L, D = (4, 256, D_MODEL)
        lim = 1.0 / np.sqrt(D)

        def lin(k):
            kw, kb = jax.random.split(k)
            W = jax.random.uniform(kw, (D, D), jnp.float32, -lim, lim)
            b = jax.random.uniform(kb, (D,), jnp.float32, -lim, lim)
            return (W, b)
        Wq, bq = lin(ks[0])
        Wk, bk = lin(ks[1])
        Wv, bv = lin(ks[2])
        Wo, bo = lin(ks[3])
        x = jax.random.normal(ks[4], (B, L, D), jnp.float32)
        return {'x': x, 'Wq': Wq, 'bq': bq, 'Wk': Wk, 'bk': bk, 'Wv': Wv, 'bv': bv, 'Wo': Wo, 'bo': bo}
    _L0_attn_in = _L0_attn_setup()

    def _L0_ffn_setup():
        import jax, jax.numpy as jnp
        import numpy as np
        from jax import lax
        B, S, H = (2, 128, 128)
        I = 64
        E = 32
        TOP_K = 4
        N_GROUP = 4
        TOPK_GROUP = 2
        SCALE = 2.5
        N_SHARED = 2
        SH_I = I * N_SHARED

        def _route(tokens, router_weight, router_bias):
            logits = tokens.astype(jnp.float32) @ router_weight.astype(jnp.float32).T
            scores = jax.nn.sigmoid(logits)
            sfc = scores + router_bias[None, :]
            T = tokens.shape[0]
            grp = sfc.reshape(T, N_GROUP, E // N_GROUP)
            group_scores = lax.top_k(grp, 2)[0].sum(-1)
            _, gidx = lax.top_k(group_scores, TOPK_GROUP)
            gmask = jax.nn.one_hot(gidx, N_GROUP, dtype=sfc.dtype).sum(1)
            smask = jnp.broadcast_to(gmask[:, :, None], (T, N_GROUP, E // N_GROUP)).reshape(T, E)
            tmp = jnp.where(smask > 0, sfc, 0.0)
            _, topk_idx = lax.top_k(tmp, TOP_K)
            topk_w = jnp.take_along_axis(scores, topk_idx, axis=1)
            topk_w = topk_w / (topk_w.sum(-1, keepdims=True) + 1e-20)
            topk_w = topk_w * SCALE
            return (topk_idx, topk_w)
        key = jax.random.key(seed)
        ks = jax.random.split(key, 10)
        std = 0.02
        return {'hidden_states': jax.random.normal(ks[0], (B, S, H), jnp.float32), 'router_weight': jax.random.normal(ks[1], (E, H), jnp.float32) * std, 'router_bias': jnp.zeros((E,), jnp.float32), 'gate_w': jax.random.normal(ks[2], (E, I, H), jnp.float32) * std, 'up_w': jax.random.normal(ks[3], (E, I, H), jnp.float32) * std, 'down_w': jax.random.normal(ks[4], (E, H, I), jnp.float32) * std, 'shared_gate_w': jax.random.normal(ks[5], (SH_I, H), jnp.float32) * std, 'shared_up_w': jax.random.normal(ks[6], (SH_I, H), jnp.float32) * std, 'shared_down_w': jax.random.normal(ks[7], (H, SH_I), jnp.float32) * std}
    _L0_ffn_in = _L0_ffn_setup()
    _d = {'L0_attn_x': _L0_attn_in['x'], 'L0_attn_Wq': _L0_attn_in['Wq'], 'L0_attn_bq': _L0_attn_in['bq'], 'L0_attn_Wk': _L0_attn_in['Wk'], 'L0_attn_bk': _L0_attn_in['bk'], 'L0_attn_Wv': _L0_attn_in['Wv'], 'L0_attn_bv': _L0_attn_in['bv'], 'L0_attn_Wo': _L0_attn_in['Wo'], 'L0_attn_bo': _L0_attn_in['bo'], 'L0_ffn_router_weight': _L0_ffn_in['router_weight'], 'L0_ffn_router_bias': _L0_ffn_in['router_bias'], 'L0_ffn_gate_w': _L0_ffn_in['gate_w'], 'L0_ffn_up_w': _L0_ffn_in['up_w'], 'L0_ffn_down_w': _L0_ffn_in['down_w'], 'L0_ffn_shared_gate_w': _L0_ffn_in['shared_gate_w'], 'L0_ffn_shared_up_w': _L0_ffn_in['shared_up_w'], 'L0_ffn_shared_down_w': _L0_ffn_in['shared_down_w']}
    _x0 = _d['L0_attn_x']
    _d['L0_attn_x'] = jax.random.normal(jax.random.fold_in(jax.random.key(seed), 1), (32, 256, 128), dtype=_x0.dtype)
    del _x0
    return _d

def reference(L0_attn_x, L0_attn_Wq, L0_attn_bq, L0_attn_Wk, L0_attn_bk, L0_attn_Wv, L0_attn_bv, L0_attn_Wo, L0_attn_bo, L0_ffn_router_weight, L0_ffn_router_bias, L0_ffn_gate_w, L0_ffn_up_w, L0_ffn_down_w, L0_ffn_shared_gate_w, L0_ffn_shared_up_w, L0_ffn_shared_down_w):

    def _L0_attn_ref(x, Wq, bq, Wk, bk, Wv, bv, Wo, bo):
        import jax, jax.numpy as jnp
        import numpy as np
        D_MODEL = 128
        NHEAD = 16
        HEAD_DIM = D_MODEL // NHEAD
        MAX_POS = 256

        def _rope_tables(seq_len, dim):
            inv_freq = 1.0 / 10000.0 ** (jnp.arange(0, dim, 2, dtype=jnp.float32) / dim)
            t = jnp.arange(seq_len, dtype=jnp.float32)[:, None]
            freqs = t * inv_freq[None, :]
            emb = jnp.concatenate([freqs, freqs], axis=-1)
            return (jnp.cos(emb), jnp.sin(emb))

        def _rotate_half(x):
            x1, x2 = jnp.split(x, 2, axis=-1)
            return jnp.concatenate([-x2, x1], axis=-1)

        def _apply_rope(x, cos, sin):
            c = cos[None, :, None, :]
            s = sin[None, :, None, :]
            return x * c + _rotate_half(x) * s
        B, L, D = x.shape
        H, hd = (NHEAD, HEAD_DIM)
        q = (x @ Wq.T + bq).reshape(B, L, H, hd)
        k = (x @ Wk.T + bk).reshape(B, L, H, hd)
        v = (x @ Wv.T + bv).reshape(B, L, H, hd)
        cos, sin = _rope_tables(L, hd)
        q = _apply_rope(q, cos, sin)
        k = _apply_rope(k, cos, sin)
        scores = jnp.einsum('bqhd,bkhd->bhqk', q, k) / np.sqrt(hd).astype(np.float32)
        attn = jax.nn.softmax(scores, axis=-1)
        out = jnp.einsum('bhqk,bkhd->bqhd', attn, v).reshape(B, L, D)
        return out @ Wo.T + bo

    def _L0_ffn_ref(hidden_states, router_weight, router_bias, gate_w, up_w, down_w, shared_gate_w, shared_up_w, shared_down_w):
        import jax, jax.numpy as jnp
        import numpy as np
        from jax import lax
        B, S, H = (2, 128, 128)
        I = 64
        E = 32
        TOP_K = 4
        N_GROUP = 4
        TOPK_GROUP = 2
        SCALE = 2.5
        N_SHARED = 2
        SH_I = I * N_SHARED

        def _route(tokens, router_weight, router_bias):
            logits = tokens.astype(jnp.float32) @ router_weight.astype(jnp.float32).T
            scores = jax.nn.sigmoid(logits)
            sfc = scores + router_bias[None, :]
            T = tokens.shape[0]
            grp = sfc.reshape(T, N_GROUP, E // N_GROUP)
            group_scores = lax.top_k(grp, 2)[0].sum(-1)
            _, gidx = lax.top_k(group_scores, TOPK_GROUP)
            gmask = jax.nn.one_hot(gidx, N_GROUP, dtype=sfc.dtype).sum(1)
            smask = jnp.broadcast_to(gmask[:, :, None], (T, N_GROUP, E // N_GROUP)).reshape(T, E)
            tmp = jnp.where(smask > 0, sfc, 0.0)
            _, topk_idx = lax.top_k(tmp, TOP_K)
            topk_w = jnp.take_along_axis(scores, topk_idx, axis=1)
            topk_w = topk_w / (topk_w.sum(-1, keepdims=True) + 1e-20)
            topk_w = topk_w * SCALE
            return (topk_idx, topk_w)
        tokens = hidden_states.reshape(-1, H)
        topk_idx, topk_w = _route(tokens, router_weight, router_bias)
        gate_vals = jax.nn.silu(jnp.einsum('th,eih->tei', tokens, gate_w))
        up_vals = jnp.einsum('th,eih->tei', tokens, up_w)
        hidden_vals = gate_vals * up_vals
        expert_out = jnp.einsum('tei,ehi->teh', hidden_vals, down_w)
        sel = jnp.take_along_axis(expert_out, topk_idx[:, :, None], axis=1)
        mixed = (sel * topk_w[:, :, None].astype(sel.dtype)).sum(1)
        mixed = mixed.reshape(hidden_states.shape)
        sg = jax.nn.silu(jnp.einsum('bsh,ih->bsi', hidden_states, shared_gate_w))
        su = jnp.einsum('bsh,ih->bsi', hidden_states, shared_up_w)
        shared = jnp.einsum('bsi,hi->bsh', sg * su, shared_down_w)
        return mixed + shared
    x = L0_attn_x
    xn = _layernorm(x, axis=-1)
    x = x + _L0_attn_ref(xn, L0_attn_Wq, L0_attn_bq, L0_attn_Wk, L0_attn_bk, L0_attn_Wv, L0_attn_bv, L0_attn_Wo, L0_attn_bo) + _L0_ffn_ref(xn, L0_ffn_router_weight, L0_ffn_router_bias, L0_ffn_gate_w, L0_ffn_up_w, L0_ffn_down_w, L0_ffn_shared_gate_w, L0_ffn_shared_up_w, L0_ffn_shared_down_w)
    return x

_drawn_inputs = setup_inputs


def setup_inputs(seed=0):
    import zlib

    import numpy as np

    out = dict(_drawn_inputs(seed))
    spreads = {'L0_ffn_router_bias': (0.0, 0.8)}
    factors = {'L0_attn_Wq': 6.097,
     'L0_attn_bq': 27.882,
     'L0_attn_Wk': 6.037,
     'L0_attn_bk': 30.964,
     'L0_ffn_router_weight': 8.0,
     'L0_ffn_gate_w': 8.0,
     'L0_ffn_up_w': 8.0,
     'L0_ffn_down_w': 8.0,
     'L0_ffn_shared_gate_w': 8.0,
     'L0_ffn_shared_up_w': 8.0,
     'L0_ffn_shared_down_w': 8.0,
     'L0_attn_bv': 8.0,
     'L0_attn_bo': 5.744}
    for name, (base, spread) in spreads.items():
        noise = np.random.default_rng([zlib.crc32(name.encode()), seed]).standard_normal(out[name].shape)
        drawn = base * np.exp(spread * noise) if base else spread * noise
        out[name] = jnp.asarray(drawn.astype(out[name].dtype))
    for name, factor in factors.items():
        out[name] = (out[name] * factor).astype(out[name].dtype)
    return out
```

```python
from contextlib import ExitStack

import concourse.bass as bass
import numpy as np
from concourse import mybir

F32 = mybir.dt.float32
F32R = mybir.dt.float32r
BF16 = mybir.dt.bfloat16
U32 = mybir.dt.uint32
ALU = mybir.AluOpType
ACT = mybir.ActivationFunctionType
AX = mybir.AxisListType

P = 128
D = 128
L = 256
HEADS = 16
HD = D // HEADS
E = 32
EI = 64
PAIRS = E // 2
NG = 4
GE = E // NG
TOPK = 4
SCALE = 2.5
T = 512
NB = T // L
NA = T // P
QB = L // P
HG = HEADS // 4
EPS = 1e-5
LMROW = 96


def constants():
    inv = (np.float32(1.0) / np.float32(10000.0) ** (np.arange(0, HD, 2, dtype=np.float32) / np.float32(HD))).astype(np.float32)
    freqs = np.arange(L, dtype=np.float32)[:, None] * inv[None, :]
    emb = np.concatenate([freqs, freqs], axis=-1).astype(np.float32)
    cos = np.tile(np.cos(emb).astype(np.float32).T, (HEADS, 1))
    sin = np.tile(np.sin(emb).astype(np.float32).T, (HEADS, 1))
    ident = np.eye(P, dtype=np.float32)
    sel = np.zeros((96, PAIRS, 128), np.float32)
    for part in range(3):
        for e in range(E):
            sel[32 * part + e, e // 2, (e % 2) * EI:(e % 2 + 1) * EI] = 1.0
    later = np.array([[1.0 if j > i else 0.0 for j in range(NG)] for i in range(NG)])
    early = np.array([[1.0 if j < i else 0.0 for j in range(NG)] for i in range(NG)])
    small = np.concatenate([np.arange(E), later.ravel(), early.ravel()]).astype(np.float32)
    return {
        "c_cos": cos, "c_sin": sin, "c_ident": ident,
        "c_sel": sel.reshape(96, -1), "c_small": np.tile(small, (P, 1)),
    }


def program(nc, x, Wq, bq, Wk, bk, Wv, bv, Wo, bo, router_w, router_b, gate_w, up_w, down_w,
            sgate_w, sup_w, sdown_w, c_cos, c_sin, c_ident, c_sel, c_small, out):
    B = x.shape[0]
    NTOK = B * L
    NT = NTOK // T
    NTB = NTOK // P
    assert x.shape[1] == L and x.shape[2] == D and NTOK % T == 0
    x_rows = x.rearrange("b l d -> (b l) d")
    out_rows = out.rearrange("b l d -> (b l) d")

    def rows(ap, i):
        return ap[bass.ds(i * T, T), :].rearrange("(a p) c -> p a c", p=P)

    with ExitStack() as whole:
        def sb(name, shape, dt=F32, ctx=whole):
            return ctx.enter_context(nc.sbuf_tensor(name, shape, dt))

        bank = [whole.enter_context(nc.psum_tensor(f"bank{n}", [P, 512], F32)) for n in range(8)]

        x_all = sb("x_all", [P, NTB, D])
        xnT = sb("xnT", [P, NTOK])
        wT = sb("wT", [96, NTOK], BF16)
        ident = sb("ident", [P, P])
        identb = sb("identb", [P, P], BF16)
        gT = sb("gT", [P, E * EI])
        uT = sb("uT", [P, E * EI])
        dT = sb("dT", [P, PAIRS, D])
        sh = sb("sh", [P, 3, 128])
        wT4 = sb("wT4", [P, 4, 128])
        wrot = sb("wrot", [P, 2, 128])
        bcol = sb("bcol", [P, 6])
        cos = sb("cos", [P, L])
        sin = sb("sin", [P, L])
        sel = sb("sel", [96, PAIRS, 128], BF16)

        with ExitStack() as st1:
            raw = sb("raw", [P, 3, 16, 128], ctx=st1)
            raws = sb("raws", [P, 7, 128], ctx=st1)
            rawr = sb("rawr", [E, 128], ctx=st1)
            rwT = sb("rwT", [P, E], ctx=st1)
            self32 = sb("self32", [96, PAIRS * 128], ctx=st1)
            brow = sb("brow", [1, 6, 128], ctx=st1)
            one = sb("one", [1, 1], ctx=st1)
            rbias = sb("rbias", [P, E], ctx=st1)
            small = sb("small", [P, E + 2 * NG * NG], ctx=st1)
            stats = sb("stats", [P, NTB, 6], ctx=st1)
            mean = sb("mean", [P, NTB], ctx=st1)
            var = sb("var", [P, NTB], ctx=st1)
            tmpa = sb("tmpa", [P, NTB], ctx=st1)
            tmpb = sb("tmpb", [P, NTB], ctx=st1)
            rstd = sb("rstd", [P, NTB], ctx=st1)
            xn = sb("xn", [P, 2, NA, D], ctx=st1)
            xst = sb("xst", [P, 2, T], ctx=st1)
            th = sb("th", [P, 2, NA, E], ctx=st1)
            sc = sb("sc", [P, NA, E], ctx=st1)
            sfc = sb("sfc", [P, NA, E], ctx=st1)
            m8 = sb("m8", [P, NA, NG, 8], ctx=st1)
            gs = sb("gs", [P, NA, NG], ctx=st1)
            cgt = sb("cgt", [P, NA, NG, NG], ctx=st1)
            cge = sb("cge", [P, NA, NG, NG], ctx=st1)
            rank = sb("rank", [P, NA, NG], ctx=st1)
            sf2 = sb("sf2", [P, NA, E], ctx=st1)
            t8 = sb("t8", [P, NA, 8], ctx=st1)
            i8 = sb("i8", [P, NA, 8], U32, ctx=st1)
            f8 = sb("f8", [P, NA, 8], ctx=st1)
            eq = sb("eq", [P, TOPK, NA, E], ctx=st1)
            wgt = sb("wgt", [P, NA, E], ctx=st1)
            wsum = sb("wsum", [P, NA], ctx=st1)
            pad = sb("pad", [P, 1], ctx=st1)
            w3 = sb("w3", [P, 2, NA, 3, E], BF16, ctx=st1)

            def sem(name):
                return st1.enter_context(nc.semaphore(name))

            x_in = [sem(f"x_in{n}") for n in range(8)]
            w_in = sem("w_in")
            c_in = sem("c_in")
            id_in = sem("id_in")
            one_set = sem("one_set")
            wt_done = sem("wt_done")
            wt_used = sem("wt_used")
            b_done = sem("b_done")
            const_done = sem("const_done")
            dve = sem("dve")
            var_done = sem("var_done")
            std_done = sem("std_done")
            xn_done = sem("xn_done")
            xnt_done = sem("xnt_done")
            xst_done = sem("xst_done")
            lg_done = sem("lg_done")
            th_done = sem("th_done")
            w3_done = sem("w3_done")
            w3t_done = sem("w3t_done")
            wT_done = sem("wT_done")
            xnT_done = sem("xnT_done")
            th_used = sem("th_used")

            WT_BANKS = 14
            blocks = ([("gate", n) for n in range(16)] + [("up", n) for n in range(16)]
                      + [("down", n) for n in range(16)] + [("small", n) for n in range(7)])
            groups = [blocks[4 * n:4 * n + 4] for n in range(WT_BANKS)]

            block = st1.enter_context(nc.Block())

            @block.sync
            def _(sp):
                sp.dma_start(ident[:, :], c_ident).then_inc(id_in, 16)
                sp.dma_start(raw[:, 0], gate_w.rearrange("e i h -> (e i) h").rearrange("(n p) h -> p n h", p=P)).then_inc(w_in, 16)
                sp.dma_start(raw[:, 1], up_w.rearrange("e i h -> (e i) h").rearrange("(n p) h -> p n h", p=P)).then_inc(w_in, 16)
                sp.dma_start(raw[:, 2].rearrange("p n (e i) -> p (n e) i", e=2), down_w.rearrange("e h i -> h e i")).then_inc(w_in, 16)
                for n, w in enumerate((sgate_w, sup_w, sdown_w, Wq, Wk, Wv, Wo)):
                    sp.dma_start(raws[:, n], w).then_inc(w_in, 16)
                sp.dma_start(rawr[:, :], router_w).then_inc(w_in, 16)
                w = NTB // 8
                for n in range(8):
                    sp.dma_start(x_all[:, n * w:(n + 1) * w, :],
                                 x_rows[n * w * P:(n + 1) * w * P, :].rearrange("(a p) c -> p a c", p=P)).then_inc(x_in[n], 16)

            @block.gpsimd
            def _(pool):
                pool.memset(one[:, :], 1.0).then_inc(one_set, 1)
                for n, b in enumerate((bq, bk)):
                    pool.dma_start(brow[:, n], b.rearrange("(a c) -> a c", a=1)).then_inc(c_in, 16)
                pool.dma_start(brow[:, 4], bv.rearrange("(a c) -> a c", a=1)).then_inc(c_in, 16)
                pool.dma_start(brow[:, 5], bo.rearrange("(a c) -> a c", a=1)).then_inc(c_in, 16)
                pool.dma_start(cos[:, :], c_cos).then_inc(c_in, 16)
                pool.dma_start(sin[:, :], c_sin).then_inc(c_in, 16)
                pool.dma_start(self32[:, :], c_sel).then_inc(c_in, 16)
                pool.dma_start(small[:, :], c_small).then_inc(c_in, 16)
                pool.dma_start(rbias[:, :], router_b.rearrange("(a c) -> a c", a=1).broadcast_to([P, E])).then_inc(c_in, 16)
                pool.wait_ge(c_in, 16 * 9)
                pool.wait_ge(id_in, 16)
                pool.tensor_copy(identb[:, :], ident[:, :]).then_inc(const_done, 1)
                pool.tensor_copy(sel[:, :, :].rearrange("p n c -> p (n c)"), self32[:, :]).then_inc(const_done, 1)
                for n in range(2):
                    src = brow[:, n].rearrange("a (h t d) -> a h t d", t=2, d=HD // 2)
                    dst = brow[:, 2 + n].rearrange("a (h t d) -> a h t d", t=2, d=HD // 2)
                    pool.tensor_scalar(dst[:, :, 0], src[:, :, 1], -1.0, None, ALU.mult).then_inc(const_done, 1)
                    pool.tensor_copy(dst[:, :, 1], src[:, :, 0]).then_inc(const_done, 1)
                with pool.Fori(0, NT // 2) as i:
                    for h in range(2):
                        pool.wait_ge(one_set, 1)
                        pool.wait_ge(xst_done, i * 2 + (h + 1))
                        pool.tensor_copy(xnT[:, bass.ds(i * (2 * T) + h * T, T)], xst[:, h, :]).then_inc(xnT_done, 1)

            @block.tensor
            def _(pe):
                pe.wait_ge(id_in, 16)
                pe.wait_ge(w_in, 16 * 11)
                for n, group in enumerate(groups):
                    if n >= 4:
                        pe.wait_ge(wt_used, n - 3)
                    for m, (kind, k) in enumerate(group):
                        src = raws[:, k] if kind == "small" else raw[:, ("gate", "up", "down").index(kind), k]
                        last = pe.transpose(bank[n % 4][:, 128 * m:128 * m + 128], src, ident[:, :])
                    last.then_inc(wt_done, 1)
                pe.transpose(bank[4][:, 0:E], rawr[:, :], ident[0:E, 0:E]).then_inc(b_done, 1)
                pe.wait_ge(one_set, 1)
                pe.wait_ge(const_done, 6)
                for n in range(6):
                    last = pe.matmul(bank[5][:, n:n + 1], brow[:, n], one[:, :], start=True, stop=True)
                last.then_inc(b_done, 1)

                def transpose_xn(i, h):
                    pe.wait_ge(xn_done, i * 2 + (h + 1))
                    pe.wait_ge(xst_done, i * 2 + h if h else i * 2)
                    for a in range(NA):
                        last = pe.transpose(bank[6][:, a * P:a * P + P], xn[:, h, a, :], ident[:, :])
                    last.then_inc(xnt_done, 1)

                def logits(i, h):
                    pe.wait_ge(xst_done, i * 2 + (h + 1))
                    pe.wait_ge(th_done, i * 2 + h)
                    for a in range(NA):
                        last = pe.matmul(bank[7][:, a * E:a * E + E], xst[:, h, a * P:a * P + P], rwT[:, :],
                                         start=True, stop=True)
                    last.then_inc(lg_done, 1)

                def transpose_w(i, h):
                    pe.wait_ge(w3_done, i * 2 + (h + 1))
                    pe.wait_ge(wT_done, i * 2 + h)
                    for a in range(NA):
                        last = pe.transpose(bank[4].bitcast(BF16)[0:96, a * P:a * P + P],
                                            w3[:, h, a].rearrange("p k e -> p (k e)"), identb[:, :])
                    last.then_inc(w3t_done, 1)

                pe.wait_ge(wt_used, WT_BANKS + 3)
                with pe.Fori(0, NT // 2) as i:
                    for h in range(2):
                        transpose_xn(i, h)
                        logits(i, h)
                    for h in range(2):
                        transpose_w(i, h)

            @block.scalar
            def _(act):
                for n, group in enumerate(groups):
                    act.wait_ge(wt_done, n + 1)
                    if n < 12:
                        dst = (gT[:, :], uT[:, :], dT[:, :, :].rearrange("p n c -> p (n c)"))[n // 4]
                        dst = dst[:, (n % 4) * 512:(n % 4) * 512 + 512]
                        act.activation(dst, bank[n % 4][:, :], ACT.Copy).then_inc(wt_used, 1)
                    elif n == 12:
                        act.activation(sh[:, :, :].rearrange("p n c -> p (n c)"), bank[n % 4][:, 0:384], ACT.Copy).then_inc(wt_used, 1)
                        act.activation(wT4[:, 0], bank[n % 4][:, 384:512], ACT.Copy).then_inc(wt_used, 1)
                    else:
                        act.activation(wT4[:, 1:4].rearrange("p n c -> p (n c)"), bank[n % 4][:, 0:384], ACT.Copy).then_inc(wt_used, 1)
                act.wait_ge(b_done, 1)
                act.activation(rwT[:, :], bank[4][:, 0:E], ACT.Copy).then_inc(wt_used, 1)
                act.wait_ge(b_done, 2)
                act.activation(bcol[:, :], bank[5][:, 0:6], ACT.Copy).then_inc(wt_used, 1)
                act.wait_ge(var_done, 1)
                act.activation(tmpb[:, :], tmpa[:, :], ACT.Sqrt).then_inc(std_done, 1)
                with act.Fori(0, NT // 2) as i:
                    for h in range(2):
                        act.wait_ge(xnt_done, i * 2 + (h + 1))
                        act.wait_ge(xnT_done, i * 2)
                        act.wait_ge(lg_done, i * 2)
                        act.activation(xst[:, h, :], bank[6][:, :], ACT.Copy).then_inc(xst_done, 1)
                        act.wait_ge(lg_done, i * 2 + (h + 1))
                        act.wait_ge(th_used, i * 2)
                        act.activation(th[:, h].rearrange("p a e -> p (a e)"), bank[7][:, 0:NA * E], ACT.Tanh, scale=0.5).then_inc(th_done, 1)

            @block.vector
            def _(v):
                n_dve = [0]

                def link(ins):
                    n_dve[0] += 1
                    ins.then_inc(dve, 1)
                    v.wait_ge(dve, n_dve[0])

                for n in range(8):
                    v.wait_ge(x_in[n], 16)
                    for a in range(n * NTB // 8, (n + 1) * NTB // 8):
                        last = v.bn_stats(stats[:, a, :], x_all[:, a, :])
                link(last)
                link(v.tensor_tensor(mean[:, :], stats[:, :, 1], stats[:, :, 4], ALU.add))
                link(v.tensor_scalar(mean[:, :], mean[:, :], 0.5, None, ALU.mult))
                link(v.tensor_tensor(tmpa[:, :], stats[:, :, 1], mean[:, :], ALU.subtract))
                link(v.tensor_tensor(tmpa[:, :], tmpa[:, :], tmpa[:, :], ALU.mult))
                link(v.tensor_tensor(var[:, :], stats[:, :, 2], stats[:, :, 5], ALU.add))
                link(v.scalar_tensor_tensor(var[:, :], var[:, :], 1.0 / D, tmpa[:, :], ALU.mult, ALU.add))
                v.tensor_scalar(tmpa[:, :], var[:, :], EPS, None, ALU.add).then_inc(var_done, 1)
                v.wait_ge(std_done, 1)
                v.wait_ge(var_done, 1)
                link(v.reciprocal(rstd[:, :], tmpb[:, :]))
                link(v.tensor_tensor(tmpb[:, :], rstd[:, :], rstd[:, :], ALU.mult))
                link(v.tensor_tensor(tmpb[:, :], tmpb[:, :], tmpa[:, :], ALU.mult))
                link(v.tensor_scalar(tmpb[:, :], tmpb[:, :], -0.5, 1.5, ALU.mult, ALU.add))
                link(v.tensor_tensor(rstd[:, :], rstd[:, :], tmpb[:, :], ALU.mult))
                v.wait_ge(wt_used, WT_BANKS + 3)
                for n in range(2):
                    src = wT4[:, n].rearrange("p (h t d) -> p h t d", t=2, d=HD // 2)
                    dst = wrot[:, n].rearrange("p (h t d) -> p h t d", t=2, d=HD // 2)
                    v.tensor_scalar(dst[:, :, 0], src[:, :, 1], -1.0, None, ALU.mult)
                    v.tensor_copy(dst[:, :, 1], src[:, :, 0])
                v.wait_ge(c_in, 16 * 9)

                base = n_dve[0]
                per = [0]
                cur = [None]
                PER = 2 * 24

                def step(ins, fixed=False):
                    per[0] += 1
                    ins.then_inc(dve, 1)
                    v.wait_ge(dve, cur[0] * PER + (base + per[0]))
                    if fixed:
                        v.memset(pad[:, :], 0.0)

                def normalise(i, h):
                    v.wait_ge(xnt_done, i * 2)
                    for a in range(NA):
                        k = i * (2 * NA) + (h * NA + a)
                        last = v.tensor_scalar(xn[:, h, a, :], x_all[:, bass.ds(k, 1), :].rearrange("p a c -> p (a c)"),
                                               mean[:, bass.ds(k, 1)], rstd[:, bass.ds(k, 1)], ALU.subtract, ALU.mult)
                    last.then_inc(xn_done, 1)

                def route(i, h):
                    cur[0] = i
                    v.wait_ge(th_done, i * 2 + (h + 1))
                    link_ = step
                    link_(v.tensor_scalar(sc[:, :, :], th[:, h], 0.5, 0.5, ALU.mult, ALU.add))
                    link_(v.tensor_tensor(sfc[:, :, :], sc[:, :, :], rbias[:, :].unsqueeze(1).broadcast_to([P, NA, E]), ALU.add), fixed=True)
                    for a in range(NA):
                        for g in range(NG):
                            last = v.max(m8[:, a, g, :], sfc[:, a, g * GE:(g + 1) * GE])
                    link_(last)
                    link_(v.tensor_tensor(gs[:, :, :], m8[:, :, :, 0], m8[:, :, :, 1], ALU.add))
                    si = gs[:, :, :].unsqueeze(3).broadcast_to([P, NA, NG, NG])
                    sj = gs[:, :, :].unsqueeze(2).broadcast_to([P, NA, NG, NG])
                    lt = small[:, E:E + NG * NG].rearrange("p (i j) -> p i j", i=NG).unsqueeze(1).broadcast_to([P, NA, NG, NG])
                    er = small[:, E + NG * NG:E + 2 * NG * NG].rearrange("p (i j) -> p i j", i=NG).unsqueeze(1).broadcast_to([P, NA, NG, NG])
                    v.tensor_tensor(cgt[:, :, :, :], sj, si, ALU.is_gt)
                    link_(v.tensor_tensor(cge[:, :, :, :], sj, si, ALU.is_ge))
                    v.tensor_tensor(cgt[:, :, :, :], cgt[:, :, :, :], lt, ALU.mult)
                    link_(v.tensor_tensor(cge[:, :, :, :], cge[:, :, :, :], er, ALU.mult))
                    link_(v.tensor_tensor(cgt[:, :, :, :], cgt[:, :, :, :], cge[:, :, :, :], ALU.add))
                    link_(v.tensor_reduce(rank[:, :, :], cgt[:, :, :, :], AX.X, ALU.add))
                    link_(v.tensor_scalar(rank[:, :, :], rank[:, :, :], 2.0, None, ALU.is_lt))
                    link_(v.tensor_tensor(sf2[:, :, :].rearrange("p a (g e) -> p a g e", g=NG),
                                          sfc[:, :, :].rearrange("p a (g e) -> p a g e", g=NG),
                                          rank[:, :, :].unsqueeze(3).broadcast_to([P, NA, NG, GE]), ALU.mult), fixed=True)
                    for a in range(NA):
                        last = v.max(t8[:, a, :], sf2[:, a, :])
                    link_(last, fixed=True)
                    for a in range(NA):
                        last = v.max_index(i8[:, a, :], t8[:, a, :], sf2[:, a, :])
                    link_(last)
                    link_(v.tensor_copy(f8[:, :, :], i8[:, :, :]))
                    for k in range(TOPK):
                        last = v.tensor_tensor(eq[:, k], small[:, 0:E].unsqueeze(1).broadcast_to([P, NA, E]),
                                               f8[:, :, k:k + 1].broadcast_to([P, NA, E]), ALU.is_equal)
                    link_(last)
                    v.tensor_tensor(eq[:, 0], eq[:, 0], eq[:, 1], ALU.add)
                    link_(v.tensor_tensor(eq[:, 2], eq[:, 2], eq[:, 3], ALU.add))
                    link_(v.tensor_tensor(eq[:, 0], eq[:, 0], eq[:, 2], ALU.add))
                    link_(v.tensor_tensor(wgt[:, :, :], eq[:, 0], sc[:, :, :], ALU.mult))
                    v.tensor_reduce(wsum[:, :], wgt[:, :, :], AX.X, ALU.add).then_inc(th_used, 1)
                    return

                def weights(i, h):
                    v.wait_ge(th_used, i * 2 + (h + 1))
                    step(v.tensor_scalar(wsum[:, :], wsum[:, :], 1e-20, None, ALU.add))
                    step(v.reciprocal(wsum[:, :], wsum[:, :]))
                    step(v.scalar_tensor_tensor(wgt[:, :, :], wgt[:, :, :], SCALE, wsum[:, :].unsqueeze(2).broadcast_to([P, NA, E]), ALU.mult, ALU.mult))
                    v.wait_ge(w3t_done, i * 2)
                    step(v.tensor_copy(w3[:, h, :, 0, :], wgt[:, :, :]))
                    step(v.tensor_tensor(wgt[:, :, :], wgt[:, :, :], w3[:, h, :, 0, :], ALU.subtract))
                    step(v.tensor_copy(w3[:, h, :, 1, :], wgt[:, :, :]))
                    step(v.tensor_tensor(wgt[:, :, :], wgt[:, :, :], w3[:, h, :, 1, :], ALU.subtract))
                    v.tensor_copy(w3[:, h, :, 2, :], wgt[:, :, :]).then_inc(w3_done, 1)

                PER = 2 * 24
                with v.Fori(0, NT // 2) as i:
                    per[0] = 0
                    for h in range(2):
                        normalise(i, h)
                    for h in range(2):
                        route(i, h)
                        weights(i, h)
                    for h in range(2):
                        v.wait_ge(w3t_done, i * 2 + (h + 1))
                        v.tensor_copy(wT[:, bass.ds(i * (2 * T) + h * T, T)], bank[4].bitcast(BF16)[0:96, 0:T]).then_inc(wT_done, 1)
                    assert per[0] == PER, per[0]

        with ExitStack() as st2:
            QM = [sb(f"QM{b}", [P, HEADS, L], F32R, st2) for b in range(NB)]
            KS = [sb(f"KS{b}", [P, HG, L], F32R, st2) for b in range(NB)]
            qk1 = sb("qk1", [P, 2, T], F32R, st2)
            qk2 = sb("qk2", [P, 2, T], F32R, st2)
            ropea = sb("ropea", [P, T], ctx=st2)
            ropeb = sb("ropeb", [P, T], ctx=st2)
            qkf = sb("qkf", [P, T], ctx=st2)
            xst2 = sb("xst2", [P, T], ctx=st2)
            V = sb("V", [P, NA, HEADS, 32], ctx=st2)
            MX = sb("MX", [P, QB, HEADS], ctx=st2)
            NM = sb("NM", [HEADS, L], F32R, st2)
            NPT = 4
            PT = sb("PT", [P, NPT, T], ctx=st2)
            OT = sb("OT", [P, HG, L], ctx=st2)
            rs = sb("rs", [P, HEADS], ctx=st2)
            ON = sb("ON", [P, HEADS, HD], ctx=st2)
            OTn = sb("OTn", [P, T], ctx=st2)
            tg = sb("tg", [P, T], ctx=st2)
            hh = sb("hh", [P, T], ctx=st2)
            YT = sb("YT", [P, T], ctx=st2)

            def sem(name):
                return st2.enter_context(nc.semaphore(name))

            cleared = sem("cleared")
            xs_done = sem("xs_done")
            proj_done = sem("proj_done")
            rope_done = sem("rope_done")
            rope_used = sem("rope_used")
            qkf_done = sem("qkf_done")
            first_done = sem("first_done")
            second_done = sem("second_done")
            q_in = [sem(f"q_in{b}") for b in range(NB)]
            k_in = [sem(f"k_in{b}") for b in range(NB)]
            v_done = sem("v_done")
            v_used = sem("v_used")
            mx_done = sem("mx_done")
            mx_used = sem("mx_used")
            nmT_done = sem("nmT_done")
            nm_done = sem("nm_done")
            m_in = [sem(f"m_in{b}") for b in range(NB)]
            s_done = sem("s_done")
            p_done = sem("p_done")
            pv_done = sem("pv_done")
            ot_done = sem("ot_done")
            otT_done = sem("otT_done")
            rs_done = sem("rs_done")
            on_done = sem("on_done")
            onT_done = sem("onT_done")
            otn_done = sem("otn_done")
            y_done = sem("y_done")
            yt_done = sem("yt_done")
            ytT_done = sem("ytT_done")
            res_done = sem("res_done")
            g_done = sem("g_done")
            t_done = sem("t_done")
            h1_done = sem("h1_done")
            h_done = sem("h_done")

            block = st2.enter_context(nc.Block())
            MXB, SB, PVB, RA, RB = bank[0:2], bank[2:4], bank[4:6], bank[6], bank[7]

            @block.gpsimd
            def _(pool):
                for b in range(NB):
                    pool.memset(QM[b][:, :, :].bitcast(F32), 0.0).then_inc(cleared, 1)
                    pool.memset(KS[b][:, :, :].bitcast(F32), 0.0).then_inc(cleared, 1)
                pool.memset(V[:, :, :, :], 0.0).then_inc(cleared, 1)
                pool.wait_ge(cleared, 5)
                for b in range(NB):
                    pool.memset(KS[b][LMROW:LMROW + 1, :, :].bitcast(F32), 1.0).then_inc(cleared, 1)
                pool.wait_ge(cleared, 7)
                pool.memset(V[:, :, :, HD:HD + 1], 1.0).then_inc(cleared, 1)
                with pool.Fori(0, NT) as i:
                    pool.wait_ge(cleared, 8)
                    pool.wait_ge(v_done, i * 1)
                    pool.wait_ge(g_done, i * 1)
                    pool.tensor_copy(xst2[:, :], xnT[:, bass.ds(i * T, T)]).then_inc(xs_done, 1)
                    for n in range(2):
                        pool.wait_ge(rope_done, i * 2 + (n + 1))
                        if n == 0:
                            pool.wait_ge(q_in[0], i * (16 * 48))
                            pool.wait_ge(q_in[1], i * (16 * 48))
                            pool.wait_ge(k_in[0], i * (16 * 12))
                            pool.wait_ge(k_in[1], i * (16 * 12))
                        pool.wait_ge(second_done, i * 2 + n)
                        pool.tensor_tensor(qkf[:, :], ropea[:, :], ropeb[:, :], ALU.add).then_inc(qkf_done, 1)
                        pool.wait_ge(cleared, 8)
                        pool.wait_ge(qkf_done, i * 2 + (n + 1))
                        pool.tensor_copy(qk1[:, n, :], qkf[:, :]).then_inc(first_done, 1)
                        pool.wait_ge(first_done, i * 2 + (n + 1))
                        pool.tensor_tensor(qk2[:, n, :], qkf[:, :], qk1[:, n, :].bitcast(F32), ALU.subtract).then_inc(second_done, 1)

            @block.sync
            def _(sp):
                sp.wait_ge(cleared, 8)
                f = lambda ap: ap.bitcast(F32)
                with sp.Fori(0, NT) as i:
                    for b in range(NB):
                        cols = slice(b * L, (b + 1) * L)
                        sp.wait_ge(s_done, i * 32)
                        sp.wait_ge(second_done, i * 2 + 2)
                        for t, src in enumerate((qk1, qk1, qk2)):
                            for h in range(HEADS):
                                r = 32 * t + 8 * (h % 4)
                                sp.dma_start(f(QM[b][r:r + 8, h, :]), f(src[8 * h:8 * h + 8, 0, cols])).then_inc(q_in[b], 16)
                        for t, src in enumerate((qk1, qk2, qk1)):
                            for g in range(HG):
                                sp.dma_start(f(KS[b][32 * t:32 * t + 32, g, :]), f(src[32 * g:32 * g + 32, 1, cols])).then_inc(k_in[b], 16)
                    for b in range(NB):
                        sp.wait_ge(nm_done, i * 2 + (b + 1))
                        for h in range(HEADS):
                            sp.dma_start(f(QM[b][LMROW:LMROW + 1, h, :]), f(NM[h:h + 1, :])).then_inc(m_in[b], 16)

            @block.tensor
            def _(pe):
                pe.wait_ge(cleared, 8)

                def project(i):
                    xr = xnT[:, bass.ds(i * T, T)]
                    for n in range(2):
                        if n == 0:
                            pe.wait_ge(res_done, i * 1)
                        else:
                            pe.wait_ge(rope_done, i * 2 + 1)
                        pe.matmul(RA[:, :], wT4[:, n], xr, start=True, stop=True)
                        pe.matmul(RB[:, :], wrot[:, n], xr, start=True, stop=True).then_inc(proj_done, 1)
                    pe.wait_ge(xs_done, i * 1 + 1)
                    pe.wait_ge(rope_done, i * 2 + 2)
                    for a in range(NA):
                        last = pe.matmul(RA[:, a * P:a * P + P], xst2[:, a * P:a * P + P], wT4[:, 2], start=True, stop=True)
                    last.then_inc(v_done, 1)

                def maxima(i, b, n):
                    k = 16 * b + n
                    if n == 0:
                        pe.wait_ge(q_in[b], i * (16 * 48) + 16 * 48)
                        pe.wait_ge(k_in[b], i * (16 * 12) + 16 * 12)
                    if k >= 2:
                        pe.wait_ge(mx_used, i * 32 + (k - 1))
                    else:
                        pe.wait_ge(mx_used, i * 32 + 0)
                    for q in range(QB):
                        last = pe.matmul(MXB[k % 2][:, q * L:(q + 1) * L], QM[b][0:LMROW, n, q * P:q * P + P],
                                         KS[b][0:LMROW, n // 4, :], start=True, stop=True)
                    last.then_inc(mx_done, 1)

                def scores(i, b, n):
                    g, kb, hp = n // 4, (n // 2) % 2, n % 2
                    k = 16 * b + n
                    if n == 0:
                        pe.wait_ge(m_in[b], i * (16 * 16) + 16 * 16)
                    if k >= 2:
                        pe.wait_ge(p_done, i * 32 + (k - 1))
                    else:
                        pe.wait_ge(p_done, i * 32 + 0)
                    h = 4 * g + 2 * hp
                    pe.matmul(SB[k % 2][:, :], KS[b][0:LMROW + 1, g, kb * P:kb * P + P],
                              QM[b][0:LMROW + 1, h:h + 2, :].rearrange("p h c -> p (h c)"),
                              start=True, stop=True).then_inc(s_done, 1)

                def values(i, b, n):
                    g, kb, hp = n // 4, (n // 2) % 2, n % 2
                    k = 16 * b + n
                    if n == 0:
                        pe.wait_ge(v_used, i * 1 + 1)
                        pe.wait_ge(ot_done, i * 4 + 2 * b)
                    pe.wait_ge(p_done, i * 32 + (k + 1))
                    for e in range(2):
                        j = 2 * hp + e
                        last = pe.matmul(PVB[g // 2][32 * j:32 * j + 32, (g % 2) * L:(g % 2 + 1) * L],
                                         V[:, QB * b + kb, 4 * g + j, :], PT[:, k % NPT, e * L:(e + 1) * L],
                                         start=(kb == 0), stop=(kb == 1))
                    last.then_inc(pv_done, 1)

                def turn_max(i, b):
                    pe.wait_ge(mx_used, i * 32 + 16 * (b + 1))
                    if b == 0:
                        pe.wait_ge(v_used, i * 1 + 1)
                    else:
                        pe.wait_ge(otn_done, i * 2 + 1)
                    for q in range(QB):
                        last = pe.transpose(RA[0:HEADS, q * P:q * P + P], MX[:, q, :], ident[:, :])
                    last.then_inc(nmT_done, 1)

                def outputs(i, b):
                    pe.wait_ge(ot_done, i * 4 + (2 * b + 2))
                    for q in range(QB):
                        if q == 1:
                            pe.wait_ge(on_done, i * 4 + (2 * b + 1))
                        for g in range(HG):
                            last = pe.transpose(RB[:, g * P:g * P + P], OT[:, g, q * P:q * P + P], ident[:, :])
                        last.then_inc(otT_done, 1)
                        pe.wait_ge(on_done, i * 4 + (2 * b + q + 1))
                        if q == 0 and b == 1:
                            pe.wait_ge(nm_done, i * 2 + 2)
                        if q == 0 and b == 0:
                            pe.wait_ge(nm_done, i * 2 + 1)
                        last = pe.transpose(RA[:, q * P:q * P + P], ON[:, :, :].rearrange("p h d -> p (h d)"), ident[:, :])
                    last.then_inc(onT_done, 1)

                def finish(i):
                    pe.wait_ge(otn_done, i * 2 + 2)
                    xr = xst2[:, :]
                    pe.matmul(RA[:, :], sh[:, 0], xr, start=True, stop=True)
                    pe.matmul(RB[:, :], sh[:, 1], xr, start=True, stop=True).then_inc(g_done, 1)
                    pe.wait_ge(mx_used, i * 32 + 32)
                    pe.matmul(MXB[0][:, :], wT4[:, 3], OTn[:, :], start=True, stop=False)
                    pe.wait_ge(h_done, i * 1 + 1)
                    pe.matmul(MXB[0][:, :], sh[:, 2], hh[:, :], start=False, stop=True).then_inc(y_done, 1)
                    pe.wait_ge(yt_done, i * 1 + 1)
                    for a in range(NA):
                        last = pe.transpose(RA[:, a * P:a * P + P], YT[:, a * P:a * P + P], ident[:, :])
                    last.then_inc(ytT_done, 1)

                with pe.Fori(0, NT) as i:
                    project(i)
                    for n in range(16):
                        maxima(i, 0, n)
                    turn_max(i, 0)
                    for b in range(NB):
                        for n in range(18):
                            if n < 16:
                                scores(i, b, n)
                            if n < 16 and b == 0:
                                maxima(i, 1, n)
                            if n >= 2:
                                values(i, b, n - 2)
                        outputs(i, b)
                        if b == 0:
                            turn_max(i, 1)
                    finish(i)

            @block.scalar
            def _(act):
                def exps(i, b, n):
                    k = 16 * b + n
                    act.wait_ge(s_done, i * 32 + (k + 1))
                    if k >= NPT:
                        act.wait_ge(pv_done, i * 32 + (k - NPT + 1))
                    else:
                        act.wait_ge(pv_done, i * 32)
                    act.activation(PT[:, k % NPT, :], SB[k % 2][:, :], ACT.Exp, scale=1.0 / float(np.sqrt(np.float32(HD)))).then_inc(p_done, 1)

                def negmax(i, b):
                    act.wait_ge(nmT_done, i * 2 + (b + 1))
                    if b == 0:
                        act.wait_ge(m_in[1], i * (16 * 16))
                    else:
                        act.wait_ge(m_in[0], i * (16 * 16) + 16 * 16)
                    act.activation(NM[:, :], RA[0:HEADS, 0:L], ACT.Copy, scale=-1.0).then_inc(nm_done, 1)

                def outs(i, b):
                    for k in range(2):
                        act.wait_ge(pv_done, i * 32 + (16 * b + 8 * (k + 1)))
                        if k == 0:
                            act.wait_ge(otT_done, i * 4 + 2 * b)
                        act.activation(OT[:, 2 * k:2 * k + 2, :].rearrange("p g c -> p (g c)"), PVB[k][:, :], ACT.Copy).then_inc(ot_done, 1)

                def outs_t(i, b):
                    act.wait_ge(onT_done, i * 2 + (b + 1))
                    if b == 0:
                        act.wait_ge(y_done, i * 1)
                    act.activation(OTn[:, b * L:(b + 1) * L], RA[:, 0:L], ACT.Identity, bias=bcol[:, 4:5]).then_inc(otn_done, 1)

                with act.Fori(0, NT) as i:
                    act.wait_ge(v_done, i * 1 + 1)
                    act.wait_ge(pv_done, i * 32)
                    act.activation(V[:, :, :, 0:HD].rearrange("p a h d -> p a h d"),
                                   RA[:, :].rearrange("p (a h d) -> p a h d", a=NA, h=HEADS), ACT.Copy).then_inc(v_used, 1)
                    negmax(i, 0)
                    for b in range(NB):
                        for n in range(16):
                            exps(i, b, n)
                        outs(i, b)
                        outs_t(i, b)
                        if b == 0:
                            negmax(i, 1)
                    act.wait_ge(g_done, i * 1 + 1)
                    act.wait_ge(h1_done, i * 1)
                    act.activation(tg[:, :], RA[:, :], ACT.Tanh, scale=0.5).then_inc(t_done, 1)
                    act.wait_ge(y_done, i * 1 + 1)
                    act.wait_ge(ytT_done, i * 1)
                    act.activation(YT[:, :], MXB[0][:, :], ACT.Identity, bias=bcol[:, 5:6]).then_inc(yt_done, 1)

            @block.vector
            def _(v):
                def rope(i):
                    for n in range(2):
                        v.wait_ge(proj_done, i * 2 + (n + 1))
                        v.wait_ge(qkf_done, i * 2 + n)
                        c3 = cos[:, :].unsqueeze(1).broadcast_to([P, NB, L])
                        s3 = sin[:, :].unsqueeze(1).broadcast_to([P, NB, L])
                        r3 = lambda ap: ap[:, :].rearrange("p (b l) -> p b l", b=NB)
                        v.scalar_tensor_tensor(r3(ropea), r3(RA), bcol[:, n:n + 1], c3, ALU.add, ALU.mult)
                        v.scalar_tensor_tensor(r3(ropeb), r3(RB), bcol[:, 2 + n:3 + n], s3, ALU.add, ALU.mult).then_inc(rope_done, 1)

                def maxima(i, b, n):
                    k = 16 * b + n
                    v.wait_ge(mx_done, i * 32 + (k + 1))
                    if n == 0:
                        v.wait_ge(nmT_done, i * 2 + b)
                    v.tensor_reduce(MX[:, :, n], MXB[k % 2][:, :].rearrange("p (q c) -> p q c", q=QB), AX.X, ALU.max).then_inc(mx_used, 1)

                def divide(i, b):
                    for q in range(QB):
                        k = 2 * b + q
                        v.wait_ge(otT_done, i * 4 + (k + 1))
                        o4 = RB[:, :].rearrange("p (h c) -> p h c", h=HEADS)
                        v.wait_ge(on_done, i * 4 + k)
                        v.reciprocal(rs[:, :], o4[:, :, HD]).then_inc(rs_done, 1)
                        v.wait_ge(rs_done, i * 4 + (k + 1))
                        if q == 0:
                            v.wait_ge(onT_done, i * 2 + b)
                        v.tensor_tensor(ON[:, :, :], o4[:, :, 0:HD], rs[:, :].unsqueeze(2).broadcast_to([P, HEADS, HD]), ALU.mult).then_inc(on_done, 1)

                with v.Fori(0, NT) as i:
                    rope(i)
                    for b in range(NB):
                        for n in range(16):
                            maxima(i, b, n)
                    for b in range(NB):
                        divide(i, b)
                    v.wait_ge(t_done, i * 1 + 1)
                    v.scalar_tensor_tensor(tg[:, :], tg[:, :], 1.0, RA[:, :], ALU.add, ALU.mult).then_inc(h1_done, 1)
                    v.wait_ge(h1_done, i * 1 + 1)
                    v.scalar_tensor_tensor(hh[:, :], tg[:, :], 0.5, RB[:, :], ALU.mult, ALU.mult).then_inc(h_done, 1)
                    v.wait_ge(ytT_done, i * 1 + 1)
                    xa = x_all[:, bass.ds(i * NA, NA), :].rearrange("p a c -> p (a c)")
                    v.tensor_tensor(xa, RA[:, :], xa, ALU.add).then_inc(res_done, 1)

        with ExitStack() as st3:
            tg3 = sb("tg3", [P, 2, T], ctx=st3)
            ha = sb("ha", [P, 2, T], ctx=st3)
            hb = sb("hb", [P, 2, T], ctx=st3)
            hw = sb("hw", [P, 2, T], ctx=st3)
            yt3 = sb("yt3", [P, T], ctx=st3)

            def sem(name):
                return st3.enter_context(nc.semaphore(name))

            gu_done = sem("gu_done")
            t3_done = sem("t3_done")
            ha_done = sem("ha_done")
            hb_done = sem("hb_done")
            hw_done = sem("hw_done")
            dn_done = sem("dn_done")
            y3_done = sem("y3_done")
            y3T_done = sem("y3T_done")
            r3_done = sem("r3_done")
            stored = sem("stored")
            block = st3.enter_context(nc.Block())
            GB, UB, WB, YB, TB = bank[0:2], bank[2:4], bank[4:6], bank[6], bank[7]

            @block.tensor
            def _(pe):
                with pe.Fori(0, NT) as i:
                    xr = xnT[:, bass.ds(i * T, T)]
                    wr = wT[:, bass.ds(i * T, T)]

                    def up(p):
                        cols = slice(p * 128, p * 128 + 128)
                        pe.wait_ge(hw_done, i * PAIRS + (p - 1) if p >= 2 else i * PAIRS)
                        pe.matmul(GB[p % 2][:, :], gT[:, cols], xr, start=True, stop=True)
                        pe.matmul(UB[p % 2][:, :], uT[:, cols], xr, start=True, stop=True)
                        pe.matmul(WB[p % 2][:, :], sel[:, p, :], wr, start=True, stop=True).then_inc(gu_done, 1)

                    def down(p):
                        pe.wait_ge(hw_done, i * PAIRS + (p + 1))
                        if p == 0:
                            pe.wait_ge(y3_done, i * 1)
                        pe.matmul(YB[:, :], dT[:, p, :], hw[:, p % 2, :], start=(p == 0), stop=(p == PAIRS - 1)).then_inc(dn_done, 1)

                    for p in range(PAIRS + 1):
                        if p < PAIRS:
                            up(p)
                        if p >= 1:
                            down(p - 1)
                    pe.wait_ge(y3_done, i * 1 + 1)
                    pe.wait_ge(r3_done, i * 1)
                    for a in range(NA):
                        last = pe.transpose(TB[:, a * P:a * P + P], yt3[:, a * P:a * P + P], ident[:, :])
                    last.then_inc(y3T_done, 1)

            @block.scalar
            def _(act):
                with act.Fori(0, NT) as i:
                    for p in range(PAIRS):
                        act.wait_ge(gu_done, i * PAIRS + (p + 1))
                        act.wait_ge(ha_done, i * PAIRS + (p - 1) if p >= 2 else i * PAIRS)
                        act.activation(tg3[:, p % 2, :], GB[p % 2][:, :], ACT.Tanh, scale=0.5).then_inc(t3_done, 1)
                    act.wait_ge(dn_done, i * PAIRS + PAIRS)
                    act.wait_ge(y3T_done, i * 1)
                    act.activation(yt3[:, :], YB[:, :], ACT.Copy).then_inc(y3_done, 1)

            @block.vector
            def _(v):
                with v.Fori(0, NT) as i:
                    for p in range(PAIRS):
                        k = p % 2
                        v.wait_ge(t3_done, i * PAIRS + (p + 1))
                        v.scalar_tensor_tensor(ha[:, k, :], tg3[:, k, :], 1.0, GB[k][:, :], ALU.add, ALU.mult).then_inc(ha_done, 1)
                        v.wait_ge(ha_done, i * PAIRS + (p + 1))
                        v.scalar_tensor_tensor(hb[:, k, :], ha[:, k, :], 0.5, UB[k][:, :], ALU.mult, ALU.mult).then_inc(hb_done, 1)
                        v.wait_ge(hb_done, i * PAIRS + (p + 1))
                        v.wait_ge(dn_done, i * PAIRS + (p - 1) if p >= 2 else i * PAIRS)
                        v.tensor_tensor(hw[:, k, :], hb[:, k, :], WB[k][:, :], ALU.mult).then_inc(hw_done, 1)
                    v.wait_ge(y3T_done, i * 1 + 1)
                    xa = x_all[:, bass.ds(i * NA, NA), :].rearrange("p a c -> p (a c)")
                    v.tensor_tensor(xa, TB[:, :], xa, ALU.add).then_inc(r3_done, 1)

            @block.sync
            def _(sp):
                with sp.Fori(0, NT) as i:
                    sp.wait_ge(r3_done, i * 1 + 1)
                    sp.dma_start(rows(out_rows, i), x_all[:, bass.ds(i * NA, NA), :]).then_inc(stored, 16)
                sp.wait_ge(stored, 16 * NT)


_INS = ["L0_attn_x", "L0_attn_Wq", "L0_attn_bq", "L0_attn_Wk", "L0_attn_bk", "L0_attn_Wv", "L0_attn_bv",
        "L0_attn_Wo", "L0_attn_bo", "L0_ffn_router_weight", "L0_ffn_router_bias", "L0_ffn_gate_w", "L0_ffn_up_w",
        "L0_ffn_down_w", "L0_ffn_shared_gate_w", "L0_ffn_shared_up_w", "L0_ffn_shared_down_w"]


def kernel(**inputs):
    import concourse.bacc as bacc
    from concourse.bass_utils import run_bass_kernel_spmd

    nc = bacc.Bacc("TRN2", target_bir_lowering=False, num_devices=1)
    arrays = {name: np.ascontiguousarray(inputs[name]) for name in _INS}
    arrays.update(constants())
    args = [nc.dram_tensor(f"in_{name}", a.shape, mybir.dt.from_np(a.dtype), kind="ExternalInput").ap()
            for name, a in arrays.items()]
    out = nc.dram_tensor("out_y", arrays["L0_attn_x"].shape, F32, kind="ExternalOutput").ap()
    program(nc, *args, out)
    r = run_bass_kernel_spmd(nc, [{f"in_{name}": a for name, a in arrays.items()}], core_ids=[0])
    return r.results[0]["out_y"]
```

```python
from contextlib import ExitStack

import concourse.bass as bass
import numpy as np
from concourse import mybir

F32 = mybir.dt.float32
F32R = mybir.dt.float32r
BF16 = mybir.dt.bfloat16
U32 = mybir.dt.uint32
ALU = mybir.AluOpType
ACT = mybir.ActivationFunctionType
AX = mybir.AxisListType

P = 128
D = 128
L = 256
HEADS = 16
HD = D // HEADS
E = 32
EI = 64
PAIRS = E // 2
NG = 4
GE = E // NG
TOPK = 4
SCALE = 2.5
T = 512
NB = T // L
NA = T // P
QB = L // P
HG = HEADS // 4
EPS = 1e-5
UNITS = NB * 4
LAG = 3
LMROW = 96


def constants():
    inv = (np.float32(1.0) / np.float32(10000.0) ** (np.arange(0, HD, 2, dtype=np.float32) / np.float32(HD))).astype(np.float32)
    freqs = np.arange(L, dtype=np.float32)[:, None] * inv[None, :]
    emb = np.concatenate([freqs, freqs], axis=-1).astype(np.float32)
    cos = np.tile(np.cos(emb).astype(np.float32).T, (HEADS, 1))
    sin = np.tile(np.sin(emb).astype(np.float32).T, (HEADS, 1))
    ident = np.eye(P, dtype=np.float32)
    sel = np.zeros((96, PAIRS, 128), np.float32)
    for part in range(3):
        for e in range(E):
            sel[32 * part + e, e // 2, (e % 2) * EI:(e % 2 + 1) * EI] = 1.0
    later = np.array([[1.0 if j > i else 0.0 for j in range(NG)] for i in range(NG)])
    early = np.array([[1.0 if j < i else 0.0 for j in range(NG)] for i in range(NG)])
    small = np.concatenate([np.arange(E), later.ravel(), early.ravel()]).astype(np.float32)
    mask = np.array([[1.0 if (r % 32) // HD == j else 0.0 for j in range(4)] for r in range(96)], np.float32)
    return {
        "c_cos": cos, "c_sin": sin, "c_ident": ident,
        "c_sel": sel.reshape(96, -1), "c_small": np.tile(small, (P, 1)),
        "c_mask": mask,
    }


def program(nc, x, Wq, bq, Wk, bk, Wv, bv, Wo, bo, router_w, router_b, gate_w, up_w, down_w,
            sgate_w, sup_w, sdown_w, c_cos, c_sin, c_ident, c_sel, c_small, c_mask, out):
    B = x.shape[0]
    NTOK = B * L
    NT = NTOK // T
    NTB = NTOK // P
    assert x.shape[1] == L and x.shape[2] == D and NTOK % T == 0
    x_rows = x.rearrange("b l d -> (b l) d")
    out_rows = out.rearrange("b l d -> (b l) d")

    def rows(ap, i):
        return ap[bass.ds(i * T, T), :].rearrange("(a p) c -> p a c", p=P)

    with ExitStack() as whole:
        def sb(name, shape, dt=F32, ctx=whole):
            return ctx.enter_context(nc.sbuf_tensor(name, shape, dt))

        bank = [whole.enter_context(nc.psum_tensor(f"bank{n}", [P, 512], F32)) for n in range(8)]

        x_all = sb("x_all", [P, NTB, D])
        xnT = sb("xnT", [P, NTOK])
        wT = sb("wT", [96, NTOK], BF16)
        ident = sb("ident", [P, P])
        identb = sb("identb", [P, P], BF16)
        gT = sb("gT", [P, E * EI])
        uT = sb("uT", [P, E * EI])
        dT = sb("dT", [P, PAIRS, D])
        sh = sb("sh", [P, 3, 128])
        wT4 = sb("wT4", [P, 4, 128])
        wrot = sb("wrot", [P, 2, 128])
        bcol = sb("bcol", [P, 6])
        cos = sb("cos", [P, L])
        sin = sb("sin", [P, L])
        sel = sb("sel", [96, PAIRS, 128], BF16)

        with ExitStack() as st1:
            raw = sb("raw", [P, 3, 16, 128], ctx=st1)
            raws = sb("raws", [P, 7, 128], ctx=st1)
            rawr = sb("rawr", [E, 128], ctx=st1)
            rwT = sb("rwT", [P, E], ctx=st1)
            self32 = sb("self32", [96, PAIRS * 128], ctx=st1)
            brow = sb("brow", [1, 6, 128], ctx=st1)
            one = sb("one", [1, 1], ctx=st1)
            rbias = sb("rbias", [P, E], ctx=st1)
            small = sb("small", [P, E + 2 * NG * NG], ctx=st1)
            stats = sb("stats", [P, NTB, 6], ctx=st1)
            mean = sb("mean", [P, NTB], ctx=st1)
            var = sb("var", [P, NTB], ctx=st1)
            tmpa = sb("tmpa", [P, NTB], ctx=st1)
            tmpb = sb("tmpb", [P, NTB], ctx=st1)
            rstd = sb("rstd", [P, NTB], ctx=st1)
            xn = sb("xn", [P, 2, NA, D], ctx=st1)
            xst = sb("xst", [P, 2, T], ctx=st1)
            th = sb("th", [P, 2, NA, E], ctx=st1)
            sc = sb("sc", [P, NA, E], ctx=st1)
            sfc = sb("sfc", [P, NA, E], ctx=st1)
            m8 = sb("m8", [P, NA, NG, 8], ctx=st1)
            gs = sb("gs", [P, NA, NG], ctx=st1)
            cgt = sb("cgt", [P, NA, NG, NG], ctx=st1)
            cge = sb("cge", [P, NA, NG, NG], ctx=st1)
            rank = sb("rank", [P, NA, NG], ctx=st1)
            sf2 = sb("sf2", [P, NA, E], ctx=st1)
            t8 = sb("t8", [P, NA, 8], ctx=st1)
            i8 = sb("i8", [P, NA, 8], U32, ctx=st1)
            f8 = sb("f8", [P, NA, 8], ctx=st1)
            eq = sb("eq", [P, TOPK, NA, E], ctx=st1)
            wgt = sb("wgt", [P, NA, E], ctx=st1)
            wsum = sb("wsum", [P, NA], ctx=st1)
            pad = sb("pad", [P, 1], ctx=st1)
            w3 = sb("w3", [P, 2, NA, 3, E], BF16, ctx=st1)

            def sem(name):
                return st1.enter_context(nc.semaphore(name))

            x_in = [sem(f"x_in{n}") for n in range(8)]
            w_in = sem("w_in")
            c_in = sem("c_in")
            id_in = sem("id_in")
            one_set = sem("one_set")
            wt_done = sem("wt_done")
            wt_used = sem("wt_used")
            b_done = sem("b_done")
            const_done = sem("const_done")
            dve = sem("dve")
            var_done = sem("var_done")
            std_done = sem("std_done")
            xn_done = sem("xn_done")
            xnt_done = sem("xnt_done")
            xst_done = sem("xst_done")
            lg_done = sem("lg_done")
            th_done = sem("th_done")
            w3_done = sem("w3_done")
            w3t_done = sem("w3t_done")
            wT_done = sem("wT_done")
            xnT_done = sem("xnT_done")
            th_used = sem("th_used")

            WT_BANKS = 14
            blocks = ([("gate", n) for n in range(16)] + [("up", n) for n in range(16)]
                      + [("down", n) for n in range(16)] + [("small", n) for n in range(7)])
            groups = [blocks[4 * n:4 * n + 4] for n in range(WT_BANKS)]

            block = st1.enter_context(nc.Block())

            @block.sync
            def _(sp):
                sp.dma_start(ident[:, :], c_ident).then_inc(id_in, 16)
                sp.dma_start(raw[:, 0], gate_w.rearrange("e i h -> (e i) h").rearrange("(n p) h -> p n h", p=P)).then_inc(w_in, 16)
                sp.dma_start(raw[:, 1], up_w.rearrange("e i h -> (e i) h").rearrange("(n p) h -> p n h", p=P)).then_inc(w_in, 16)
                sp.dma_start(raw[:, 2].rearrange("p n (e i) -> p (n e) i", e=2), down_w.rearrange("e h i -> h e i")).then_inc(w_in, 16)
                for n, w in enumerate((sgate_w, sup_w, sdown_w, Wq, Wk, Wv, Wo)):
                    sp.dma_start(raws[:, n], w).then_inc(w_in, 16)
                sp.dma_start(rawr[:, :], router_w).then_inc(w_in, 16)
                w = NTB // 8
                for n in range(8):
                    sp.dma_start(x_all[:, n * w:(n + 1) * w, :],
                                 x_rows[n * w * P:(n + 1) * w * P, :].rearrange("(a p) c -> p a c", p=P)).then_inc(x_in[n], 16)

            @block.gpsimd
            def _(pool):
                pool.memset(one[:, :], 1.0).then_inc(one_set, 1)
                for n, b in enumerate((bq, bk)):
                    pool.dma_start(brow[:, n], b.rearrange("(a c) -> a c", a=1)).then_inc(c_in, 16)
                pool.dma_start(brow[:, 4], bv.rearrange("(a c) -> a c", a=1)).then_inc(c_in, 16)
                pool.dma_start(brow[:, 5], bo.rearrange("(a c) -> a c", a=1)).then_inc(c_in, 16)
                pool.dma_start(cos[:, :], c_cos).then_inc(c_in, 16)
                pool.dma_start(sin[:, :], c_sin).then_inc(c_in, 16)
                pool.dma_start(self32[:, :], c_sel).then_inc(c_in, 16)
                pool.dma_start(small[:, :], c_small).then_inc(c_in, 16)
                pool.dma_start(rbias[:, :], router_b.rearrange("(a c) -> a c", a=1).broadcast_to([P, E])).then_inc(c_in, 16)
                pool.wait_ge(c_in, 16 * 9)
                pool.wait_ge(id_in, 16)
                pool.tensor_copy(identb[:, :], ident[:, :]).then_inc(const_done, 1)
                pool.tensor_copy(sel[:, :, :].rearrange("p n c -> p (n c)"), self32[:, :]).then_inc(const_done, 1)
                for n in range(2):
                    src = brow[:, n].rearrange("a (h t d) -> a h t d", t=2, d=HD // 2)
                    dst = brow[:, 2 + n].rearrange("a (h t d) -> a h t d", t=2, d=HD // 2)
                    pool.tensor_scalar(dst[:, :, 0], src[:, :, 1], -1.0, None, ALU.mult).then_inc(const_done, 1)
                    pool.tensor_copy(dst[:, :, 1], src[:, :, 0]).then_inc(const_done, 1)
                with pool.Fori(0, NT // 2) as i:
                    for h in range(2):
                        pool.wait_ge(one_set, 1)
                        pool.wait_ge(xst_done, i * 2 + (h + 1))
                        pool.tensor_copy(xnT[:, bass.ds(i * (2 * T) + h * T, T)], xst[:, h, :]).then_inc(xnT_done, 1)

            @block.tensor
            def _(pe):
                pe.wait_ge(id_in, 16)
                pe.wait_ge(w_in, 16 * 11)
                for n, group in enumerate(groups):
                    if n >= 4:
                        pe.wait_ge(wt_used, n - 3)
                    for m, (kind, k) in enumerate(group):
                        src = raws[:, k] if kind == "small" else raw[:, ("gate", "up", "down").index(kind), k]
                        last = pe.transpose(bank[n % 4][:, 128 * m:128 * m + 128], src, ident[:, :])
                    last.then_inc(wt_done, 1)
                pe.transpose(bank[4][:, 0:E], rawr[:, :], ident[0:E, 0:E]).then_inc(b_done, 1)
                pe.wait_ge(one_set, 1)
                pe.wait_ge(const_done, 6)
                for n in range(6):
                    last = pe.matmul(bank[5][:, n:n + 1], brow[:, n], one[:, :], start=True, stop=True)
                last.then_inc(b_done, 1)

                def transpose_xn(i, h):
                    pe.wait_ge(xn_done, i * 2 + (h + 1))
                    pe.wait_ge(xst_done, i * 2 + h if h else i * 2)
                    for a in range(NA):
                        last = pe.transpose(bank[6][:, a * P:a * P + P], xn[:, h, a, :], ident[:, :])
                    last.then_inc(xnt_done, 1)

                def logits(i, h):
                    pe.wait_ge(xst_done, i * 2 + (h + 1))
                    pe.wait_ge(th_done, i * 2 + h)
                    for a in range(NA):
                        last = pe.matmul(bank[7][:, a * E:a * E + E], xst[:, h, a * P:a * P + P], rwT[:, :],
                                         start=True, stop=True)
                    last.then_inc(lg_done, 1)

                def transpose_w(i, h):
                    pe.wait_ge(w3_done, i * 2 + (h + 1))
                    pe.wait_ge(wT_done, i * 2 + h)
                    for a in range(NA):
                        last = pe.transpose(bank[4].bitcast(BF16)[0:96, a * P:a * P + P],
                                            w3[:, h, a].rearrange("p k e -> p (k e)"), identb[:, :])
                    last.then_inc(w3t_done, 1)

                pe.wait_ge(wt_used, WT_BANKS + 3)
                with pe.Fori(0, NT // 2) as i:
                    for h in range(2):
                        transpose_xn(i, h)
                        logits(i, h)
                    for h in range(2):
                        transpose_w(i, h)

            @block.scalar
            def _(act):
                for n, group in enumerate(groups):
                    act.wait_ge(wt_done, n + 1)
                    if n < 12:
                        dst = (gT[:, :], uT[:, :], dT[:, :, :].rearrange("p n c -> p (n c)"))[n // 4]
                        dst = dst[:, (n % 4) * 512:(n % 4) * 512 + 512]
                        act.activation(dst, bank[n % 4][:, :], ACT.Copy).then_inc(wt_used, 1)
                    elif n == 12:
                        act.activation(sh[:, :, :].rearrange("p n c -> p (n c)"), bank[n % 4][:, 0:384], ACT.Copy).then_inc(wt_used, 1)
                        act.activation(wT4[:, 0], bank[n % 4][:, 384:512], ACT.Copy).then_inc(wt_used, 1)
                    else:
                        act.activation(wT4[:, 1:4].rearrange("p n c -> p (n c)"), bank[n % 4][:, 0:384], ACT.Copy).then_inc(wt_used, 1)
                act.wait_ge(b_done, 1)
                act.activation(rwT[:, :], bank[4][:, 0:E], ACT.Copy).then_inc(wt_used, 1)
                act.wait_ge(b_done, 2)
                act.activation(bcol[:, :], bank[5][:, 0:6], ACT.Copy).then_inc(wt_used, 1)
                act.wait_ge(var_done, 1)
                act.activation(tmpb[:, :], tmpa[:, :], ACT.Sqrt).then_inc(std_done, 1)
                with act.Fori(0, NT // 2) as i:
                    for h in range(2):
                        act.wait_ge(xnt_done, i * 2 + (h + 1))
                        act.wait_ge(xnT_done, i * 2)
                        act.wait_ge(lg_done, i * 2)
                        act.activation(xst[:, h, :], bank[6][:, :], ACT.Copy).then_inc(xst_done, 1)
                        act.wait_ge(lg_done, i * 2 + (h + 1))
                        act.wait_ge(th_used, i * 2)
                        act.activation(th[:, h].rearrange("p a e -> p (a e)"), bank[7][:, 0:NA * E], ACT.Tanh, scale=0.5).then_inc(th_done, 1)

            @block.vector
            def _(v):
                n_dve = [0]

                def link(ins):
                    n_dve[0] += 1
                    ins.then_inc(dve, 1)
                    v.wait_ge(dve, n_dve[0])

                for n in range(8):
                    v.wait_ge(x_in[n], 16)
                    for a in range(n * NTB // 8, (n + 1) * NTB // 8):
                        last = v.bn_stats(stats[:, a, :], x_all[:, a, :])
                link(last)
                link(v.tensor_tensor(mean[:, :], stats[:, :, 1], stats[:, :, 4], ALU.add))
                link(v.tensor_scalar(mean[:, :], mean[:, :], 0.5, None, ALU.mult))
                link(v.tensor_tensor(tmpa[:, :], stats[:, :, 1], mean[:, :], ALU.subtract))
                link(v.tensor_tensor(tmpa[:, :], tmpa[:, :], tmpa[:, :], ALU.mult))
                link(v.tensor_tensor(var[:, :], stats[:, :, 2], stats[:, :, 5], ALU.add))
                link(v.scalar_tensor_tensor(var[:, :], var[:, :], 1.0 / D, tmpa[:, :], ALU.mult, ALU.add))
                v.tensor_scalar(tmpa[:, :], var[:, :], EPS, None, ALU.add).then_inc(var_done, 1)
                v.wait_ge(std_done, 1)
                v.wait_ge(var_done, 1)
                link(v.reciprocal(rstd[:, :], tmpb[:, :]))
                link(v.tensor_tensor(tmpb[:, :], rstd[:, :], rstd[:, :], ALU.mult))
                link(v.tensor_tensor(tmpb[:, :], tmpb[:, :], tmpa[:, :], ALU.mult))
                link(v.tensor_scalar(tmpb[:, :], tmpb[:, :], -0.5, 1.5, ALU.mult, ALU.add))
                link(v.tensor_tensor(rstd[:, :], rstd[:, :], tmpb[:, :], ALU.mult))
                v.wait_ge(wt_used, WT_BANKS + 3)
                for n in range(2):
                    src = wT4[:, n].rearrange("p (h t d) -> p h t d", t=2, d=HD // 2)
                    dst = wrot[:, n].rearrange("p (h t d) -> p h t d", t=2, d=HD // 2)
                    v.tensor_scalar(dst[:, :, 0], src[:, :, 1], -1.0, None, ALU.mult)
                    v.tensor_copy(dst[:, :, 1], src[:, :, 0])
                v.wait_ge(c_in, 16 * 9)

                base = n_dve[0]
                per = [0]
                cur = [None]
                PER = 2 * 24

                def step(ins, fixed=False):
                    per[0] += 1
                    ins.then_inc(dve, 1)
                    v.wait_ge(dve, cur[0] * PER + (base + per[0]))
                    if fixed:
                        v.memset(pad[:, :], 0.0)

                def normalise(i, h):
                    v.wait_ge(xnt_done, i * 2)
                    for a in range(NA):
                        k = i * (2 * NA) + (h * NA + a)
                        last = v.tensor_scalar(xn[:, h, a, :], x_all[:, bass.ds(k, 1), :].rearrange("p a c -> p (a c)"),
                                               mean[:, bass.ds(k, 1)], rstd[:, bass.ds(k, 1)], ALU.subtract, ALU.mult)
                    last.then_inc(xn_done, 1)

                def route(i, h):
                    cur[0] = i
                    v.wait_ge(th_done, i * 2 + (h + 1))
                    link_ = step
                    link_(v.tensor_scalar(sc[:, :, :], th[:, h], 0.5, 0.5, ALU.mult, ALU.add))
                    link_(v.tensor_tensor(sfc[:, :, :], sc[:, :, :], rbias[:, :].unsqueeze(1).broadcast_to([P, NA, E]), ALU.add), fixed=True)
                    for a in range(NA):
                        for g in range(NG):
                            last = v.max(m8[:, a, g, :], sfc[:, a, g * GE:(g + 1) * GE])
                    link_(last)
                    link_(v.tensor_tensor(gs[:, :, :], m8[:, :, :, 0], m8[:, :, :, 1], ALU.add))
                    si = gs[:, :, :].unsqueeze(3).broadcast_to([P, NA, NG, NG])
                    sj = gs[:, :, :].unsqueeze(2).broadcast_to([P, NA, NG, NG])
                    lt = small[:, E:E + NG * NG].rearrange("p (i j) -> p i j", i=NG).unsqueeze(1).broadcast_to([P, NA, NG, NG])
                    er = small[:, E + NG * NG:E + 2 * NG * NG].rearrange("p (i j) -> p i j", i=NG).unsqueeze(1).broadcast_to([P, NA, NG, NG])
                    v.tensor_tensor(cgt[:, :, :, :], sj, si, ALU.is_gt)
                    link_(v.tensor_tensor(cge[:, :, :, :], sj, si, ALU.is_ge))
                    v.tensor_tensor(cgt[:, :, :, :], cgt[:, :, :, :], lt, ALU.mult)
                    link_(v.tensor_tensor(cge[:, :, :, :], cge[:, :, :, :], er, ALU.mult))
                    link_(v.tensor_tensor(cgt[:, :, :, :], cgt[:, :, :, :], cge[:, :, :, :], ALU.add))
                    link_(v.tensor_reduce(rank[:, :, :], cgt[:, :, :, :], AX.X, ALU.add))
                    link_(v.tensor_scalar(rank[:, :, :], rank[:, :, :], 2.0, None, ALU.is_lt))
                    link_(v.tensor_tensor(sf2[:, :, :].rearrange("p a (g e) -> p a g e", g=NG),
                                          sfc[:, :, :].rearrange("p a (g e) -> p a g e", g=NG),
                                          rank[:, :, :].unsqueeze(3).broadcast_to([P, NA, NG, GE]), ALU.mult), fixed=True)
                    for a in range(NA):
                        last = v.max(t8[:, a, :], sf2[:, a, :])
                    link_(last, fixed=True)
                    for a in range(NA):
                        last = v.max_index(i8[:, a, :], t8[:, a, :], sf2[:, a, :])
                    link_(last)
                    link_(v.tensor_copy(f8[:, :, :], i8[:, :, :]))
                    for k in range(TOPK):
                        last = v.tensor_tensor(eq[:, k], small[:, 0:E].unsqueeze(1).broadcast_to([P, NA, E]),
                                               f8[:, :, k:k + 1].broadcast_to([P, NA, E]), ALU.is_equal)
                    link_(last)
                    v.tensor_tensor(eq[:, 0], eq[:, 0], eq[:, 1], ALU.add)
                    link_(v.tensor_tensor(eq[:, 2], eq[:, 2], eq[:, 3], ALU.add))
                    link_(v.tensor_tensor(eq[:, 0], eq[:, 0], eq[:, 2], ALU.add))
                    link_(v.tensor_tensor(wgt[:, :, :], eq[:, 0], sc[:, :, :], ALU.mult))
                    v.tensor_reduce(wsum[:, :], wgt[:, :, :], AX.X, ALU.add).then_inc(th_used, 1)
                    return

                def weights(i, h):
                    v.wait_ge(th_used, i * 2 + (h + 1))
                    step(v.tensor_scalar(wsum[:, :], wsum[:, :], 1e-20, None, ALU.add))
                    step(v.reciprocal(wsum[:, :], wsum[:, :]))
                    step(v.scalar_tensor_tensor(wgt[:, :, :], wgt[:, :, :], SCALE, wsum[:, :].unsqueeze(2).broadcast_to([P, NA, E]), ALU.mult, ALU.mult))
                    v.wait_ge(w3t_done, i * 2)
                    step(v.tensor_copy(w3[:, h, :, 0, :], wgt[:, :, :]))
                    step(v.tensor_tensor(wgt[:, :, :], wgt[:, :, :], w3[:, h, :, 0, :], ALU.subtract))
                    step(v.tensor_copy(w3[:, h, :, 1, :], wgt[:, :, :]))
                    step(v.tensor_tensor(wgt[:, :, :], wgt[:, :, :], w3[:, h, :, 1, :], ALU.subtract))
                    v.tensor_copy(w3[:, h, :, 2, :], wgt[:, :, :]).then_inc(w3_done, 1)

                PER = 2 * 24
                with v.Fori(0, NT // 2) as i:
                    per[0] = 0
                    for h in range(2):
                        normalise(i, h)
                    for h in range(2):
                        route(i, h)
                        weights(i, h)
                    for h in range(2):
                        v.wait_ge(w3t_done, i * 2 + (h + 1))
                        v.tensor_copy(wT[:, bass.ds(i * (2 * T) + h * T, T)], bank[4].bitcast(BF16)[0:96, 0:T]).then_inc(wT_done, 1)
                    assert per[0] == PER, per[0]

        with ExitStack() as st2:
            QM = sb("QM", [P, UNITS, 4, L], F32R, st2)
            QS = [sb(f"QS{b}", [P, HG, L], F32R, st2) for b in range(NB)]
            KS = [sb(f"KS{b}", [P, HG, L], F32R, st2) for b in range(NB)]
            mask = sb("mask", [96, 4], ctx=st2)
            qk1 = sb("qk1", [P, 2, T], F32R, st2)
            qk2 = sb("qk2", [P, 2, T], F32R, st2)
            ropea = sb("ropea", [P, T], ctx=st2)
            ropeb = sb("ropeb", [P, T], ctx=st2)
            qkf = sb("qkf", [P, T], ctx=st2)
            xst2 = sb("xst2", [P, T], ctx=st2)
            V = [sb(f"V{b}", [P, QB, HEADS, 32], ctx=st2) for b in range(NB)]
            MX = sb("MX", [P, 2, 4, QB], ctx=st2)
            NM = sb("NM", [8, 2, P], F32R, st2)
            PT = sb("PT", [P, 4, T], ctx=st2)
            OT = sb("OT", [P, 2, L], ctx=st2)
            rs = sb("rs", [P, QB, 8], ctx=st2)
            ON = sb("ON", [P, QB, HEADS, HD], ctx=st2)
            OTn = sb("OTn", [P, T], ctx=st2)
            tg = sb("tg", [P, T], ctx=st2)
            hh = sb("hh", [P, T], ctx=st2)
            YT = sb("YT", [P, T], ctx=st2)
            spill = nc.dram_tensor("spill", (2, 2, P, T), F32).ap()

            def sem(name):
                return st2.enter_context(nc.semaphore(name))

            cleared = sem("cleared")
            m_tab = sem("m_tab")
            xs_done = sem("xs_done")
            proj_done = sem("proj_done")
            rope_done = sem("rope_done")
            sum_done = sem("sum_done")
            first_done = sem("first_done")
            second_done = sem("second_done")
            spilled = sem("spilled")
            q_in = [sem(f"q_in{b}") for b in range(NB)]
            k_in = [sem(f"k_in{n}") for n in range(2 * NB)]
            m_in = [sem(f"m_in{u}") for u in range(UNITS)]
            qm_done = sem("qm_done")
            v_done = sem("v_done")
            v_used = sem("v_used")
            mx_done = sem("mx_done")
            mx_used = sem("mx_used")
            nmT_done = sem("nmT_done")
            nm_done = sem("nm_done")
            s_done = sem("s_done")
            p_done = sem("p_done")
            pv_done = sem("pv_done")
            ot_done = sem("ot_done")
            otT_done = sem("otT_done")
            rs_done = sem("rs_done")
            on_done = sem("on_done")
            onT_done = sem("onT_done")
            otn_done = sem("otn_done")
            g_done = sem("g_done")
            t_done = sem("t_done")
            h1_done = sem("h1_done")
            h_done = sem("h_done")
            y_done = sem("y_done")
            yt_done = sem("yt_done")
            ytT_done = sem("ytT_done")
            res_done = sem("res_done")

            def wait(eng, s, v):
                if not isinstance(v, int) or v > 0:
                    eng.wait_ge(s, v)

            def waits(eng, *pairs):
                pairs = [(s, v if isinstance(v, int) else eng.compute_val(v)) for s, v in pairs]
                for s, v in pairs:
                    wait(eng, s, v)

            def tiles(eng, tile, first=None):
                tile(0, True, False, True)
                with eng.Fori(1, NT - 1) as i:
                    tile(i, True, True, True)
                tile(NT - 1, True, True, False)
                tile(NT, False, True, False)

            block = st2.enter_context(nc.Block())
            MXB, SB, PVB, RA, RB = bank[0:2], bank[2:4], bank[4:6], bank[6], bank[7]
            BACK, PVLAG = 4 * LAG, 2

            @block.gpsimd
            def _(pool):
                pool.dma_start(mask[:, :], c_mask).then_inc(m_tab, 16)
                for n in range(NB):
                    pool.memset(V[n][:, :, :, :], 0.0).then_inc(cleared, 1)
                pool.wait_ge(cleared, 2)
                for n in range(NB):
                    pool.memset(V[n][:, :, :, HD:HD + 1], 1.0).then_inc(cleared, 1)
                    pool.wait_ge(cleared, 3 + 2 * n)
                    pool.memset(KS[n][LMROW:LMROW + 1, :, :].bitcast(F32), 1.0).then_inc(cleared, 1)
                    pool.wait_ge(cleared, 4 + 2 * n)
                pool.wait_ge(m_tab, 16)

                def split(i):
                    for n in range(2):
                        wait(pool, rope_done, i * 2 + (n + 1))
                        wait(pool, second_done, i * 2 + n)
                        if n == 0:
                            wait(pool, spilled, i * 32)
                        pool.tensor_tensor(qkf[:, :], ropea[:, :], ropeb[:, :], ALU.add).then_inc(sum_done, 1)
                        pool.tensor_tensor(qk1[:, n, :], ropea[:, :], ropeb[:, :], ALU.add).then_inc(first_done, 1)
                        wait(pool, sum_done, i * 2 + (n + 1))
                        wait(pool, first_done, i * 2 + (n + 1))
                        pool.tensor_tensor(qk2[:, n, :], qkf[:, :], qk1[:, n, :].bitcast(F32), ALU.subtract).then_inc(second_done, 1)

                def masked(i, b):
                    wait(pool, q_in[b], i * 48 + 48)
                    for g in range(HG):
                        u = 4 * b + g
                        wait(pool, s_done, i * 32 - 32 + 4 * (u + 1))
                        pool.tensor_tensor(QM[0:96, u], QS[b][0:96, g, :].bitcast(F32).unsqueeze(1).broadcast_to([96, 4, L]),
                                           mask[:, :].unsqueeze(2).broadcast_to([96, 4, L]), ALU.mult).then_inc(qm_done, 1)

                def tile(i, now, before, after):
                    if now:
                        masked(i, 1)
                    if after:
                        split(i + 1)
                        masked(i + 1, 0)

                split(0)
                masked(0, 0)
                tiles(pool, tile)

            @block.sync
            def _(sp):
                f = lambda ap: ap.bitcast(F32)
                sp.wait_ge(cleared, 6)

                def spill_parts(i):
                    waits(sp, (second_done, i * 2 + 2), *((s, i * 48) for s in q_in + k_in))
                    for n, part in enumerate((qk1, qk2)):
                        sp.dma_start(spill[n].rearrange("m p t -> p m t"), f(part[:, :, :])).then_inc(spilled, 16)

                def load_q(i, b):
                    waits(sp, (spilled, i * 32 + 32), (qm_done, i * 8 - 8 + 4 * (b + 1)))
                    for t, part in enumerate((0, 1, 0)):
                        src = spill[part, 0, :, b * L:(b + 1) * L].rearrange("(g r) c -> r g c", g=HG)
                        sp.dma_start(f(QS[b][32 * t:32 * t + 32, :, :]), src).then_inc(q_in[b], 16)

                def load_k(i, b, half):
                    waits(sp, (spilled, i * 32 + 32), (s_done, i * 32 - 32 + 4 * (4 * b + 2 * half + 2)))
                    for t, part in enumerate((0, 0, 1)):
                        src = spill[part, 1, :, b * L:(b + 1) * L].rearrange("(g r) c -> r g c", g=HG)
                        sp.dma_start(f(KS[b][32 * t:32 * t + 32, 2 * half:2 * half + 2, :]),
                                     src[:, 2 * half:2 * half + 2, :]).then_inc(k_in[2 * b + half], 16)

                def maximum(i, u):
                    wait(sp, nm_done, i * 8 + (u + 1))
                    sp.dma_start(f(QM[LMROW:LMROW + 1, u, :, :]).rearrange("o h (q c) -> o (h q) c", q=QB),
                                 f(NM[:, u % 2, :])).then_inc(m_in[u], 16)

                def tile(i, now, before, after):
                    if before:
                        maximum(i - 1, 7)
                    if now:
                        load_k(i, 1, 0)
                        maximum(i, 0)
                        maximum(i, 1)
                        load_k(i, 1, 1)
                        maximum(i, 2)
                        maximum(i, 3)
                    if after:
                        spill_parts(i + 1)
                    if now:
                        maximum(i, 4)
                    if after:
                        load_q(i + 1, 0)
                        load_k(i + 1, 0, 0)
                    if now:
                        maximum(i, 5)
                    if after:
                        load_q(i + 1, 1)
                    if now:
                        maximum(i, 6)
                    if after:
                        load_k(i + 1, 0, 1)

                spill_parts(0)
                load_q(0, 0)
                load_k(0, 0, 0)
                load_k(0, 0, 1)
                load_q(0, 1)
                tiles(sp, tile)

            @block.tensor
            def _(pe):
                pe.wait_ge(cleared, 6)

                def project(i, n):
                    xr = xnT[:, bass.ds(i * T, T)]
                    pe.matmul(RA[:, :], wT4[:, n], xr, start=True, stop=True)
                    pe.matmul(RB[:, :], wrot[:, n], xr, start=True, stop=True).then_inc(proj_done, 1)

                def project_v(i, b):
                    wait(pe, xs_done, i + 1)
                    for a in range(QB):
                        last = pe.matmul(RA[:, a * P:a * P + P], xst2[:, (QB * b + a) * P:(QB * b + a + 1) * P], wT4[:, 2],
                                         start=True, stop=True)
                    last.then_inc(v_done, 1)

                def maxima(i, s):
                    u, h = s // 4, s % 4
                    b, g = u // 4, u % 4
                    if h == 0:
                        wait(pe, qm_done, i * 8 + (u + 1))
                        if u % 2 == 0:
                            wait(pe, k_in[u // 2], i * 48 + 48)
                    wait(pe, mx_used, i * 32 + s - 1)
                    for q in range(QB):
                        last = pe.matmul(MXB[s % 2][:, q * L:(q + 1) * L], QM[0:96, u, h, q * P:q * P + P],
                                         KS[b][0:96, g, :], start=True, stop=True)
                    last.then_inc(mx_done, 1)

                def scores(i, s):
                    u, kb, hp = s // 4, (s // 2) % 2, s % 2
                    b, g = u // 4, u % 4
                    if s % 4 == 0:
                        wait(pe, m_in[u], i * 16 + 16)
                    wait(pe, p_done, i * 32 + s - 1)
                    pe.matmul(SB[s % 2][:, :], KS[b][0:LMROW + 1, g, kb * P:kb * P + P],
                              QM[0:LMROW + 1, u, 2 * hp:2 * hp + 2, :].rearrange("p h c -> p (h c)"),
                              start=True, stop=True).then_inc(s_done, 1)

                def values(i, s):
                    u, kb, hp = s // 4, (s // 2) % 2, s % 2
                    b, g = u // 4, u % 4
                    if s % 16 == 0:
                        wait(pe, v_used, i * 2 + (b + 1))
                    if s % 8 == 0:
                        wait(pe, ot_done, i * 4 + s // 8 - 1)
                    wait(pe, p_done, i * 32 + (s + 1))
                    for e in range(2):
                        j = 2 * hp + e
                        last = pe.matmul(PVB[g // 2][32 * j:32 * j + 32, (g % 2) * L:(g % 2 + 1) * L],
                                         V[b][:, kb, 4 * g + j, :], PT[:, s % 4, e * L:(e + 1) * L],
                                         start=(kb == 0), stop=(kb == 1))
                    last.then_inc(pv_done, 1)

                def turn_max(i, u):
                    wait(pe, mx_used, i * 32 + 4 * (u + 1))
                    wait(pe, nm_done, i * 8 + u)
                    pe.transpose(RB[0:8, 0:P], MX[:, u % 2].rearrange("p h q -> p (h q)"), ident[:, :]).then_inc(nmT_done, 1)

                def turn_out(i, k):
                    wait(pe, ot_done, i * 4 + (k + 1))
                    for q in range(QB):
                        for g in range(2):
                            last = pe.transpose(RA[:, (2 * q + g) * P:(2 * q + g + 1) * P], OT[:, g, q * P:q * P + P], ident[:, :])
                    last.then_inc(otT_done, 1)

                def turn_back(i, b):
                    wait(pe, on_done, i * 4 + 2 * (b + 1))
                    for q in range(QB):
                        last = pe.transpose(RA[:, q * P:q * P + P], ON[:, q].rearrange("p h d -> p (h d)"), ident[:, :])
                    last.then_inc(onT_done, 1)

                def gate_up(i):
                    xr = xnT[:, bass.ds(i * T, T)]
                    pe.matmul(RA[:, :], sh[:, 0], xr, start=True, stop=True)
                    pe.matmul(RB[:, :], sh[:, 1], xr, start=True, stop=True).then_inc(g_done, 1)

                def finish(i):
                    wait(pe, otn_done, i * 2 + 2)
                    pe.matmul(RA[:, :], wT4[:, 3], OTn[:, :], start=True, stop=False)
                    wait(pe, h_done, i + 1)
                    pe.matmul(RA[:, :], sh[:, 2], hh[:, :], start=False, stop=True).then_inc(y_done, 1)

                def turn_y(i):
                    wait(pe, yt_done, i + 1)
                    for a in range(NA):
                        last = pe.transpose(RB[:, a * P:a * P + P], YT[:, a * P:a * P + P], ident[:, :])
                    last.then_inc(ytT_done, 1)

                def tile(i, now, before, after):
                    for s in range(32):
                        if s == 0 and before:
                            wait(pe, res_done, i - 1)
                            turn_max(i - 1, 7)
                        if s % 4 == 0 and s > 0 and now:
                            u = s // 4 - 1
                            if u in (2, 3):
                                if after:
                                    wait(pe, rope_done, i * 2 + (u + 1))
                            if u == 6:
                                wait(pe, h_done, i)
                            turn_max(i, u)
                        if now:
                            maxima(i, s)
                        k = s - BACK
                        if (k >= 0 and now) or (k < 0 and before):
                            scores(i if k >= 0 else i - 1, k % 32)
                        k = s - BACK - PVLAG
                        if (k >= 0 and now) or (k < 0 and before):
                            values(i if k >= 0 else i - 1, k % 32)
                        if s == 2 and before:
                            wait(pe, on_done, i * 4 - 2)
                            turn_back(i - 1, 0)
                        if s == 5 and now:
                            wait(pe, otn_done, i * 2 - 1)
                            project_v(i, 0)
                        if s == 7 and before:
                            if now:
                                wait(pe, v_used, i * 2 + 1)
                            else:
                                wait(pe, otn_done, i * 2 - 1)
                            turn_out(i - 1, 2)
                        if s == 9 and after:
                            wait(pe, v_used, i * 2 + 1)
                            wait(pe, on_done, i * 4 - 1)
                            wait(pe, nm_done, i * 8 + 2)
                            project(i + 1, 0)
                        if s == 13 and after:
                            wait(pe, rope_done, i * 2 + 3)
                            wait(pe, nm_done, i * 8 + 3)
                            project(i + 1, 1)
                        if s == 15 and before:
                            if after:
                                wait(pe, rope_done, i * 2 + 4)
                            else:
                                wait(pe, on_done, i * 4 - 1)
                            turn_out(i - 1, 3)
                        if s == 18 and before:
                            wait(pe, on_done, i * 4)
                            turn_back(i - 1, 1)
                        if s == 21 and now:
                            if after:
                                wait(pe, rope_done, i * 2 + 4)
                            wait(pe, otn_done, i * 2)
                            project_v(i, 1)
                        if s == 23 and now:
                            wait(pe, v_used, i * 2 + 2)
                            turn_out(i, 0)
                        if s == 25 and before:
                            if now:
                                wait(pe, on_done, i * 4 + 1)
                                wait(pe, nm_done, i * 8 + 6)
                            else:
                                wait(pe, otn_done, i * 2)
                                wait(pe, nm_done, i * 8)
                            gate_up(i - 1)
                        if s == 29 and before:
                            wait(pe, h_done, i)
                            finish(i - 1)
                        if s == 31 and before:
                            if now:
                                wait(pe, nm_done, i * 8 + 7)
                            turn_y(i - 1)
                        if s == 31 and now:
                            wait(pe, yt_done, i)
                            if not before:
                                wait(pe, on_done, i * 4 + 1)
                            turn_out(i, 1)

                project(0, 0)
                pe.wait_ge(rope_done, 1)
                project(0, 1)
                pe.wait_ge(rope_done, 2)
                tiles(pe, tile)

            @block.scalar
            def _(act):
                act.wait_ge(cleared, 6)

                def exps(i, s):
                    wait(act, s_done, i * 32 + (s + 1))
                    wait(act, pv_done, i * 32 + s - 3)
                    act.activation(PT[:, s % 4, :], SB[s % 2][:, :], ACT.Exp,
                                   scale=1.0 / float(np.sqrt(np.float32(HD)))).then_inc(p_done, 1)

                def negmax(i, u):
                    wait(act, nmT_done, i * 8 + (u + 1))
                    if u >= 2:
                        wait(act, m_in[u - 2], i * 16 + 16)
                    else:
                        wait(act, m_in[u + 6], i * 16)
                    act.activation(NM[:, u % 2, :], RB[0:8, 0:P], ACT.Copy, scale=-1.0).then_inc(nm_done, 1)

                def outs(i, k):
                    wait(act, pv_done, i * 32 + 8 * (k + 1))
                    wait(act, otT_done, i * 4 + k)
                    act.activation(OT[:, :, :].rearrange("p g c -> p (g c)"), PVB[k % 2][:, :], ACT.Copy).then_inc(ot_done, 1)

                def outs_t(i, b):
                    wait(act, onT_done, i * 2 + (b + 1))
                    if b == 0:
                        wait(act, y_done, i)
                    act.activation(OTn[:, b * L:(b + 1) * L], RA[:, 0:L], ACT.Identity, bias=bcol[:, 4:5]).then_inc(otn_done, 1)

                def vals(i, b):
                    wait(act, v_done, i * 2 + (b + 1))
                    wait(act, pv_done, i * 32 - 32 + 16 * (b + 1))
                    act.activation(V[b][:, :, :, 0:HD], RA[:, 0:L].rearrange("p (a h d) -> p a h d", a=QB, h=HEADS),
                                   ACT.Copy).then_inc(v_used, 1)

                def tile(i, now, before, after):
                    for s in range(32):
                        k = s - BACK
                        if s == 1 and before:
                            negmax(i - 1, 7)
                        if s % 4 == 1 and s > 1 and now:
                            negmax(i, s // 4 - 1)
                        if (k >= 0 and now) or (k < 0 and before):
                            exps(i if k >= 0 else i - 1, k % 32)
                        if s in (22, 30) and now:
                            outs(i, (s - 22) // 8)
                        if s in (6, 14) and before:
                            outs(i - 1, (s + 10) // 8)
                        if s == 3 and before:
                            outs_t(i - 1, 0)
                        if s == 6 and now:
                            vals(i, 0)
                        if s == 19 and before:
                            outs_t(i - 1, 1)
                        if s == 22 and now:
                            vals(i, 1)
                        if s == 26 and before:
                            wait(act, g_done, i)
                            wait(act, h_done, i - 1)
                            act.activation(tg[:, :], RA[:, :], ACT.Tanh, scale=0.5).then_inc(t_done, 1)
                        if s == 30 and before:
                            wait(act, y_done, i)
                            wait(act, ytT_done, i - 1)
                            act.activation(YT[:, :], RA[:, :], ACT.Identity, bias=bcol[:, 5:6]).then_inc(yt_done, 1)

                tiles(act, tile)

            @block.vector
            def _(v):
                v.tensor_copy(xst2[:, :], xnT[:, 0:T]).then_inc(xs_done, 1)

                def stage(i):
                    wait(v, v_done, i * 2)
                    v.tensor_copy(xst2[:, :], xnT[:, bass.ds(i * T, T)]).then_inc(xs_done, 1)

                def rope(i, n):
                    wait(v, proj_done, i * 2 + (n + 1))
                    wait(v, second_done, i * 2 + n)
                    c3 = cos[:, :].unsqueeze(1).broadcast_to([P, NB, L])
                    s3 = sin[:, :].unsqueeze(1).broadcast_to([P, NB, L])
                    r3 = lambda ap: ap.rearrange("p (b l) -> p b l", b=NB)
                    v.scalar_tensor_tensor(r3(ropea[:, :]), r3(RA[:, :]), bcol[:, n:n + 1], c3, ALU.add, ALU.mult)
                    v.scalar_tensor_tensor(r3(ropeb[:, :]), r3(RB[:, :]), bcol[:, 2 + n:3 + n], s3, ALU.add, ALU.mult).then_inc(rope_done, 1)

                def maxima(i, s):
                    u, h = s // 4, s % 4
                    wait(v, mx_done, i * 32 + (s + 1))
                    if h == 0:
                        wait(v, nmT_done, i * 8 + u - 1)
                    v.tensor_reduce(MX[:, u % 2, h, :], MXB[s % 2][:, :].rearrange("p (q c) -> p q c", q=QB), AX.X, ALU.max).then_inc(mx_used, 1)

                def divide(i, k):
                    wait(v, otT_done, i * 4 + (k + 1))
                    o4 = RA[:, :].rearrange("p (q h c) -> p q h c", q=QB, h=8)
                    v.reciprocal(rs[:, :, :], o4[:, :, :, HD]).then_inc(rs_done, 1)
                    wait(v, rs_done, i * 4 + (k + 1))
                    if k % 2 == 0:
                        wait(v, onT_done, i * 2 + k // 2)
                    half = ON[:, :, 8 * (k % 2):8 * (k % 2) + 8, :]
                    v.tensor_tensor(half, o4[:, :, :, 0:HD], rs[:, :, :].unsqueeze(3).broadcast_to([P, QB, 8, HD]), ALU.mult).then_inc(on_done, 1)

                def tile(i, now, before, after):
                    for s in range(32):
                        if s == 0 and before:
                            divide(i - 1, 1)
                        if now:
                            maxima(i, s)
                        if s == 8 and before:
                            divide(i - 1, 2)
                        if s == 10 and after:
                            rope(i + 1, 0)
                        if s == 14 and after:
                            rope(i + 1, 1)
                        if s == 16 and before:
                            divide(i - 1, 3)
                        if s == 23 and after:
                            stage(i + 1)
                        if s == 24 and now:
                            divide(i, 0)
                        if s == 27 and before:
                            wait(v, t_done, i)
                            v.scalar_tensor_tensor(tg[:, :], tg[:, :], 1.0, RA[:, :], ALU.add, ALU.mult).then_inc(h1_done, 1)
                            wait(v, h1_done, i)
                            wait(v, y_done, i - 1)
                            v.scalar_tensor_tensor(hh[:, :], tg[:, :], 0.5, RB[:, :], ALU.mult, ALU.mult).then_inc(h_done, 1)
                        if s == 31 and before:
                            wait(v, ytT_done, i)
                            k = (i - 1) * NA
                            xa = x_all[:, bass.ds(k, NA), :].rearrange("p a c -> p (a c)")
                            v.tensor_tensor(xa, RB[:, :], xa, ALU.add).then_inc(res_done, 1)

                rope(0, 0)
                rope(0, 1)
                tiles(v, tile)

        with ExitStack() as st3:
            tg3 = sb("tg3", [P, 2, T], ctx=st3)
            ha = sb("ha", [P, 2, T], ctx=st3)
            hb = sb("hb", [P, 2, T], ctx=st3)
            hw = sb("hw", [P, 2, T], ctx=st3)
            yt3 = sb("yt3", [P, T], ctx=st3)

            def sem(name):
                return st3.enter_context(nc.semaphore(name))

            gu_done = sem("gu_done")
            t3_done = sem("t3_done")
            ha_done = sem("ha_done")
            hb_done = sem("hb_done")
            hw_done = sem("hw_done")
            dn_done = sem("dn_done")
            y3_done = sem("y3_done")
            y3T_done = sem("y3T_done")
            r3_done = sem("r3_done")
            stored = sem("stored")
            block = st3.enter_context(nc.Block())
            GB, UB, WB, YB, TB = bank[0:2], bank[2:4], bank[4:6], bank[6], bank[7]

            @block.tensor
            def _(pe):
                with pe.Fori(0, NT) as i:
                    xr = xnT[:, bass.ds(i * T, T)]
                    wr = wT[:, bass.ds(i * T, T)]

                    def up(p):
                        cols = slice(p * 128, p * 128 + 128)
                        pe.wait_ge(hw_done, i * PAIRS + (p - 1) if p >= 2 else i * PAIRS)
                        pe.matmul(GB[p % 2][:, :], gT[:, cols], xr, start=True, stop=True)
                        pe.matmul(UB[p % 2][:, :], uT[:, cols], xr, start=True, stop=True)
                        pe.matmul(WB[p % 2][:, :], sel[:, p, :], wr, start=True, stop=True).then_inc(gu_done, 1)

                    def down(p):
                        pe.wait_ge(hw_done, i * PAIRS + (p + 1))
                        if p == 0:
                            pe.wait_ge(y3_done, i * 1)
                        pe.matmul(YB[:, :], dT[:, p, :], hw[:, p % 2, :], start=(p == 0), stop=(p == PAIRS - 1)).then_inc(dn_done, 1)

                    for p in range(PAIRS + 1):
                        if p < PAIRS:
                            up(p)
                        if p >= 1:
                            down(p - 1)
                    pe.wait_ge(y3_done, i * 1 + 1)
                    pe.wait_ge(r3_done, i * 1)
                    for a in range(NA):
                        last = pe.transpose(TB[:, a * P:a * P + P], yt3[:, a * P:a * P + P], ident[:, :])
                    last.then_inc(y3T_done, 1)

            @block.scalar
            def _(act):
                with act.Fori(0, NT) as i:
                    for p in range(PAIRS):
                        act.wait_ge(gu_done, i * PAIRS + (p + 1))
                        act.wait_ge(ha_done, i * PAIRS + (p - 1) if p >= 2 else i * PAIRS)
                        act.activation(tg3[:, p % 2, :], GB[p % 2][:, :], ACT.Tanh, scale=0.5).then_inc(t3_done, 1)
                    act.wait_ge(dn_done, i * PAIRS + PAIRS)
                    act.wait_ge(y3T_done, i * 1)
                    act.activation(yt3[:, :], YB[:, :], ACT.Copy).then_inc(y3_done, 1)

            @block.vector
            def _(v):
                with v.Fori(0, NT) as i:
                    for p in range(PAIRS):
                        k = p % 2
                        v.wait_ge(t3_done, i * PAIRS + (p + 1))
                        v.scalar_tensor_tensor(ha[:, k, :], tg3[:, k, :], 1.0, GB[k][:, :], ALU.add, ALU.mult).then_inc(ha_done, 1)
                        v.wait_ge(ha_done, i * PAIRS + (p + 1))
                        v.scalar_tensor_tensor(hb[:, k, :], ha[:, k, :], 0.5, UB[k][:, :], ALU.mult, ALU.mult).then_inc(hb_done, 1)
                        v.wait_ge(hb_done, i * PAIRS + (p + 1))
                        v.wait_ge(dn_done, i * PAIRS + (p - 1) if p >= 2 else i * PAIRS)
                        v.tensor_tensor(hw[:, k, :], hb[:, k, :], WB[k][:, :], ALU.mult).then_inc(hw_done, 1)
                    v.wait_ge(y3T_done, i * 1 + 1)
                    xa = x_all[:, bass.ds(i * NA, NA), :].rearrange("p a c -> p (a c)")
                    v.tensor_tensor(xa, TB[:, :], xa, ALU.add).then_inc(r3_done, 1)

            @block.sync
            def _(sp):
                with sp.Fori(0, NT) as i:
                    sp.wait_ge(r3_done, i * 1 + 1)
                    sp.dma_start(rows(out_rows, i), x_all[:, bass.ds(i * NA, NA), :]).then_inc(stored, 16)
                sp.wait_ge(stored, 16 * NT)


_INS = ["L0_attn_x", "L0_attn_Wq", "L0_attn_bq", "L0_attn_Wk", "L0_attn_bk", "L0_attn_Wv", "L0_attn_bv",
        "L0_attn_Wo", "L0_attn_bo", "L0_ffn_router_weight", "L0_ffn_router_bias", "L0_ffn_gate_w", "L0_ffn_up_w",
        "L0_ffn_down_w", "L0_ffn_shared_gate_w", "L0_ffn_shared_up_w", "L0_ffn_shared_down_w"]


def kernel(**inputs):
    import concourse.bacc as bacc
    from concourse.bass_utils import run_bass_kernel_spmd

    nc = bacc.Bacc("TRN2", target_bir_lowering=False, num_devices=1)
    arrays = {name: np.ascontiguousarray(inputs[name]) for name in _INS}
    arrays.update(constants())
    args = [nc.dram_tensor(f"in_{name}", a.shape, mybir.dt.from_np(a.dtype), kind="ExternalInput").ap()
            for name, a in arrays.items()]
    out = nc.dram_tensor("out_y", arrays["L0_attn_x"].shape, F32, kind="ExternalOutput").ap()
    program(nc, *args, out)
    r = run_bass_kernel_spmd(nc, [{f"in_{name}": a for name, a in arrays.items()}], core_ids=[0])
    return r.results[0]["out_y"]
```

```python
from contextlib import ExitStack

import concourse.bass as bass
import numpy as np
from concourse import mybir

F32 = mybir.dt.float32
F32R = mybir.dt.float32r
BF16 = mybir.dt.bfloat16
U32 = mybir.dt.uint32
ALU = mybir.AluOpType
ACT = mybir.ActivationFunctionType
AX = mybir.AxisListType

P = 128
D = 128
L = 256
HEADS = 16
HD = D // HEADS
E = 32
EI = 64
PAIRS = E // 2
NG = 4
GE = E // NG
TOPK = 4
SCALE = 2.5
T = 512
NB = T // L
NA = T // P
QB = L // P
HG = HEADS // 4
EPS = 1e-5
UNITS = NB * 4
LAG = 3
ROUTE = 25
PICKS = 3
HLAG = 3
LMROW = 96


def constants():
    inv = (np.float32(1.0) / np.float32(10000.0) ** (np.arange(0, HD, 2, dtype=np.float32) / np.float32(HD))).astype(np.float32)
    freqs = np.arange(L, dtype=np.float32)[:, None] * inv[None, :]
    emb = np.concatenate([freqs, freqs], axis=-1).astype(np.float32)
    cos = np.tile(np.cos(emb).astype(np.float32).T, (HEADS, 1))
    sin = np.tile(np.sin(emb).astype(np.float32).T, (HEADS, 1))
    ident = np.eye(P, dtype=np.float32)
    sel = np.zeros((96, PAIRS, 128), np.float32)
    for part in range(3):
        for e in range(E):
            sel[32 * part + e, e // 2, (e % 2) * EI:(e % 2 + 1) * EI] = 1.0
    later = np.array([[1.0 if j > i else 0.0 for j in range(NG)] for i in range(NG)])
    early = np.array([[1.0 if j < i else 0.0 for j in range(NG)] for i in range(NG)])
    small = np.concatenate([np.arange(E), later.ravel(), early.ravel()]).astype(np.float32)
    mask = np.array([[1.0 if (r % 32) // HD == j else 0.0 for j in range(4)] for r in range(96)], np.float32)
    return {
        "c_cos": cos, "c_sin": sin, "c_ident": ident,
        "c_sel": sel.reshape(96, -1), "c_small": np.tile(small, (P, 1)),
        "c_mask": mask,
    }


def program(nc, x, Wq, bq, Wk, bk, Wv, bv, Wo, bo, router_w, router_b, gate_w, up_w, down_w,
            sgate_w, sup_w, sdown_w, c_cos, c_sin, c_ident, c_sel, c_small, c_mask, out):
    B = x.shape[0]
    NTOK = B * L
    NT = NTOK // T
    NTB = NTOK // P
    assert x.shape[1] == L and x.shape[2] == D and NTOK % T == 0
    x_rows = x.rearrange("b l d -> (b l) d")
    out_rows = out.rearrange("b l d -> (b l) d")

    def rows(ap, i):
        return ap[bass.ds(i * T, T), :].rearrange("(a p) c -> p a c", p=P)

    def wait(eng, s, v):
        if not isinstance(v, int) or v > 0:
            eng.wait_ge(s, v)

    def waits(eng, *pairs):
        pairs = [(s, v if isinstance(v, int) else eng.compute_val(v)) for s, v in pairs]
        for s, v in pairs:
            wait(eng, s, v)

    def walk(eng, n, step):
        step(0)
        with eng.Fori(1, n - 1) as c:
            step(c)
        step(n - 1)

    def tiles(eng, tile):
        tile(0, True, False, True)
        tile(1, True, True, True)
        with eng.Fori(2, NT - 1) as i:
            tile(i, True, True, True)
        tile(NT - 1, True, True, False)
        tile(NT, False, True, False)

    with ExitStack() as whole:
        def sb(name, shape, dt=F32, ctx=whole):
            return ctx.enter_context(nc.sbuf_tensor(name, shape, dt))

        bank = [whole.enter_context(nc.psum_tensor(f"bank{n}", [P, 512], F32)) for n in range(8)]

        x_all = sb("x_all", [P, NTB, D])
        xnT = sb("xnT", [P, NTOK])
        wT = sb("wT", [96, NTOK], BF16)
        ident = sb("ident", [P, P])
        identb = sb("identb", [P, P], BF16)
        gT = sb("gT", [P, E * EI])
        uT = sb("uT", [P, E * EI])
        dT = sb("dT", [P, PAIRS, D])
        sh = sb("sh", [P, 3, 128])
        wT4 = sb("wT4", [P, 4, 128])
        wrot = sb("wrot", [P, 2, 128])
        bcol = sb("bcol", [P, 6])
        cos = sb("cos", [P, L])
        sin = sb("sin", [P, L])
        sel = sb("sel", [96, PAIRS, 128], BF16)
        rwT = sb("rwT", [P, E])
        rbias = sb("rbias", [P, E])
        small = sb("small", [P, E + 2 * NG * NG])

        with ExitStack() as st1:
            raw = sb("raw", [P, 3, 16, 128], ctx=st1)
            raws = sb("raws", [P, 7, 128], ctx=st1)
            rawr = sb("rawr", [E, 128], ctx=st1)
            selraw = sb("selraw", [96, PAIRS * 128], ctx=st1)
            brow = sb("brow", [1, 6, 128], ctx=st1)
            one = sb("one", [1, 1], ctx=st1)
            stats = sb("stats", [P, NTB, 6], ctx=st1)
            mean = sb("mean", [P, NTB], ctx=st1)
            var = sb("var", [P, NTB], ctx=st1)
            tmpa = sb("tmpa", [P, NTB], ctx=st1)
            tmpb = sb("tmpb", [P, NTB], ctx=st1)
            rstd = sb("rstd", [P, NTB], ctx=st1)
            shift = sb("shift", [P, NTB], ctx=st1)
            xn = sb("xn", [P, 4, NA, D], ctx=st1)

            def sem(name):
                return st1.enter_context(nc.semaphore(name))

            x_in = [sem(f"x_in{n}") for n in range(8)]
            w_in = sem("w_in")
            c_in = sem("c_in")
            id_in = sem("id_in")
            one_set = sem("one_set")
            wt_done = sem("wt_done")
            wt_used = [sem(f"wt_used{n}") for n in range(2)]
            b_done = sem("b_done")
            b_used = sem("b_used")
            const_done = sem("const_done")
            dve = sem("dve")
            var_done = sem("var_done")
            shift_done = sem("shift_done")
            std_done = sem("std_done")
            xn_done = [sem(f"xn_done{n}") for n in range(2)]
            xnt_done = sem("xnt_done")
            kept = [sem(f"kept{n}") for n in range(2)]

            WT_BANKS = 14
            blocks = ([("gate", n) for n in range(16)] + [("up", n) for n in range(16)]
                      + [("down", n) for n in range(16)] + [("small", n) for n in range(7)])
            groups = [blocks[4 * n:4 * n + 4] for n in range(WT_BANKS)]

            XB = bank[4:8]

            def big(n):
                dst = (gT[:, :], uT[:, :], dT[:, :, :].rearrange("p n c -> p (n c)"))[n // 4]
                return dst[:, (n % 4) * 512:(n % 4) * 512 + 512]

            block = st1.enter_context(nc.Block())

            @block.sync
            def _(sp):
                sp.dma_start(ident[:, :], c_ident).then_inc(id_in, 16)
                sp.dma_start(rawr[:, :], router_w).then_inc(id_in, 16)
                w = NTB // 8
                for n in range(8):
                    sp.dma_start(x_all[:, n * w:(n + 1) * w, :],
                                 x_rows[n * w * P:(n + 1) * w * P, :].rearrange("(a p) c -> p a c", p=P)).then_inc(x_in[n], 16)
                sp.dma_start(raw[:, 0], gate_w.rearrange("e i h -> (e i) h").rearrange("(n p) h -> p n h", p=P)).then_inc(w_in, 16)
                sp.dma_start(raw[:, 1], up_w.rearrange("e i h -> (e i) h").rearrange("(n p) h -> p n h", p=P)).then_inc(w_in, 16)
                sp.dma_start(raw[:, 2].rearrange("p n (e i) -> p (n e) i", e=2), down_w.rearrange("e h i -> h e i")).then_inc(w_in, 16)
                for n, w in enumerate((sgate_w, sup_w, sdown_w, Wq, Wk, Wv, Wo)):
                    sp.dma_start(raws[:, n], w).then_inc(w_in, 16)

            @block.gpsimd
            def _(pool):
                pool.memset(one[:, :], 1.0).then_inc(one_set, 1)
                for n, b in enumerate((bq, bk)):
                    pool.dma_start(brow[:, n], b.rearrange("(a c) -> a c", a=1)).then_inc(c_in, 16)
                pool.dma_start(brow[:, 4], bv.rearrange("(a c) -> a c", a=1)).then_inc(c_in, 16)
                pool.dma_start(brow[:, 5], bo.rearrange("(a c) -> a c", a=1)).then_inc(c_in, 16)
                pool.dma_start(cos[:, :], c_cos).then_inc(c_in, 16)
                pool.dma_start(sin[:, :], c_sin).then_inc(c_in, 16)
                pool.dma_start(selraw[:, :], c_sel).then_inc(c_in, 16)
                pool.dma_start(small[:, :], c_small).then_inc(c_in, 16)
                pool.dma_start(rbias[:, :], router_b.rearrange("(a c) -> a c", a=1).broadcast_to([P, E])).then_inc(c_in, 16)
                pool.wait_ge(c_in, 16 * 9)
                pool.wait_ge(id_in, 32)
                pool.tensor_copy(identb[:, :], ident[:, :]).then_inc(const_done, 1)
                pool.tensor_copy(sel[:, :, :].rearrange("p n c -> p (n c)"), selraw[:, :]).then_inc(const_done, 1)
                for n in range(2):
                    src = brow[:, n].rearrange("a (h t d) -> a h t d", t=2, d=HD // 2)
                    dst = brow[:, 2 + n].rearrange("a (h t d) -> a h t d", t=2, d=HD // 2)
                    pool.tensor_scalar(dst[:, :, 0], src[:, :, 1], -1.0, None, ALU.mult).then_inc(const_done, 1)
                    pool.tensor_copy(dst[:, :, 1], src[:, :, 0]).then_inc(const_done, 1)

            @block.tensor
            def _(pe):
                pe.wait_ge(id_in, 32)
                pe.transpose(bank[0][:, 0:E], rawr[:, :], ident[0:E, 0:E]).then_inc(b_done, 1)
                pe.wait_ge(b_used, 1)

                def tokens(c):
                    for j in range(4):
                        wait(pe, xn_done[j % 2], c * 2 + (j // 2 + 1))
                        wait(pe, kept[j % 2], c * 2 + (j // 2 - 1))
                        for a in range(NA):
                            last = pe.transpose(XB[j][:, a * P:a * P + P], xn[:, j, a, :], ident[:, :])
                        last.then_inc(xnt_done, 1)

                walk(pe, NT // 4, tokens)
                pe.wait_ge(kept[0], NT // 2)
                pe.wait_ge(one_set, 1)
                pe.wait_ge(const_done, 6)
                for n in range(6):
                    last = pe.matmul(bank[4][:, n:n + 1], brow[:, n], one[:, :], start=True, stop=True)
                last.then_inc(b_done, 1)
                pe.wait_ge(w_in, 16 * 10)
                for n, group in enumerate(groups):
                    if n >= 4:
                        pe.wait_ge(wt_used[n % 2], (n - 4) // 2 + 1)
                    for m, (kind, k) in enumerate(group):
                        src = raws[:, k] if kind == "small" else raw[:, ("gate", "up", "down").index(kind), k]
                        last = pe.transpose(bank[n % 4][:, 128 * m:128 * m + 128], src, ident[:, :])
                    last.then_inc(wt_done, 1)

            @block.scalar
            def _(act):
                act.wait_ge(var_done, 1)
                act.activation(tmpb[:, :], tmpa[:, :], ACT.Sqrt).then_inc(std_done, 1)
                act.wait_ge(b_done, 1)
                act.activation(rwT[:, :], bank[0][:, 0:E], ACT.Copy).then_inc(b_used, 1)

                def tokens(c):
                    for j in (0, 2):
                        wait(act, xnt_done, c * 4 + (j - 3))
                        for a in range(NA):
                            k = c * (4 * NA) + (j * NA + a)
                            last = act.activation(xn[:, j, a, :], x_all[:, bass.ds(k, 1), :].rearrange("p a c -> p (a c)"),
                                                  ACT.Identity, scale=rstd[:, bass.ds(k, 1)], bias=shift[:, bass.ds(k, 1)])
                        last.then_inc(xn_done[0], 1)
                    for j in (1, 3):
                        wait(act, xnt_done, c * 4 + (j + 1))
                        act.activation(xnT[:, bass.ds(c * (4 * T) + j * T, T)], XB[j][:, :], ACT.Copy).then_inc(kept[1], 1)

                act.wait_ge(shift_done, 1)
                walk(act, NT // 4, tokens)
                act.wait_ge(b_done, 2)
                act.activation(bcol[:, :], bank[4][:, 0:6], ACT.Copy).then_inc(b_used, 1)
                for n in range(0, 12, 2):
                    act.wait_ge(wt_done, n + 1)
                    act.activation(big(n), bank[n % 4][:, :], ACT.Copy).then_inc(wt_used[0], 1)
                act.wait_ge(wt_done, 13)
                act.activation(sh[:, :, :].rearrange("p n c -> p (n c)"), bank[0][:, 0:384], ACT.Copy)
                act.activation(wT4[:, 0], bank[0][:, 384:512], ACT.Copy).then_inc(wt_used[0], 1)

            @block.vector
            def _(v):
                n_dve = [0]

                def link(ins):
                    n_dve[0] += 1
                    ins.then_inc(dve, 1)
                    v.wait_ge(dve, n_dve[0])

                for n in range(8):
                    v.wait_ge(x_in[n], 16)
                    for a in range(n * NTB // 8, (n + 1) * NTB // 8):
                        last = v.bn_stats(stats[:, a, :], x_all[:, a, :])
                link(last)
                link(v.tensor_tensor(mean[:, :], stats[:, :, 1], stats[:, :, 4], ALU.add))
                link(v.tensor_scalar(mean[:, :], mean[:, :], 0.5, None, ALU.mult))
                link(v.tensor_tensor(tmpa[:, :], stats[:, :, 1], mean[:, :], ALU.subtract))
                link(v.tensor_tensor(tmpa[:, :], tmpa[:, :], tmpa[:, :], ALU.mult))
                link(v.tensor_tensor(var[:, :], stats[:, :, 2], stats[:, :, 5], ALU.add))
                link(v.scalar_tensor_tensor(var[:, :], var[:, :], 1.0 / D, tmpa[:, :], ALU.mult, ALU.add))
                v.tensor_scalar(tmpa[:, :], var[:, :], EPS, None, ALU.add).then_inc(var_done, 1)
                v.wait_ge(std_done, 1)
                v.wait_ge(var_done, 1)
                link(v.reciprocal(rstd[:, :], tmpb[:, :]))
                link(v.tensor_tensor(tmpb[:, :], rstd[:, :], rstd[:, :], ALU.mult))
                link(v.tensor_tensor(tmpb[:, :], tmpb[:, :], tmpa[:, :], ALU.mult))
                link(v.tensor_scalar(tmpb[:, :], tmpb[:, :], -0.5, 1.5, ALU.mult, ALU.add))
                link(v.tensor_tensor(rstd[:, :], rstd[:, :], tmpb[:, :], ALU.mult))
                v.scalar_tensor_tensor(shift[:, :], mean[:, :], -1.0, rstd[:, :], ALU.mult, ALU.mult).then_inc(shift_done, 1)

                def tokens(c):
                    for j in (1, 3):
                        wait(v, xnt_done, c * 4 + (j - 3))
                        for a in range(NA):
                            k = c * (4 * NA) + (j * NA + a)
                            last = v.tensor_scalar(xn[:, j, a, :], x_all[:, bass.ds(k, 1), :].rearrange("p a c -> p (a c)"),
                                                   mean[:, bass.ds(k, 1)], rstd[:, bass.ds(k, 1)], ALU.subtract, ALU.mult)
                        last.then_inc(xn_done[1], 1)
                    for j in (0, 2):
                        wait(v, xnt_done, c * 4 + (j + 1))
                        v.tensor_copy(xnT[:, bass.ds(c * (4 * T) + j * T, T)], XB[j][:, :]).then_inc(kept[0], 1)

                walk(v, NT // 4, tokens)
                for n in range(1, 12, 2):
                    v.wait_ge(wt_done, n + 1)
                    v.tensor_copy(big(n), bank[n % 4][:, :]).then_inc(wt_used[1], 1)
                v.wait_ge(wt_done, 14)
                v.tensor_copy(wT4[:, 1:4].rearrange("p n c -> p (n c)"), bank[1][:, 0:384]).then_inc(wt_used[1], 1)
                v.wait_ge(wt_used[0], 7)
                v.wait_ge(wt_used[1], 7)
                for n in range(2):
                    src = wT4[:, n].rearrange("p (h t d) -> p h t d", t=2, d=HD // 2)
                    dst = wrot[:, n].rearrange("p (h t d) -> p h t d", t=2, d=HD // 2)
                    v.tensor_scalar(dst[:, :, 0], src[:, :, 1], -1.0, None, ALU.mult)
                    v.tensor_copy(dst[:, :, 1], src[:, :, 0])

        with ExitStack() as st2:
            QM = sb("QM", [P, UNITS, 4, L], F32R, st2)
            QS = [sb(f"QS{b}", [P, HG, L], F32R, st2) for b in range(NB)]
            KS = [sb(f"KS{b}", [P, HG, L], F32R, st2) for b in range(NB)]
            mask = sb("mask", [96, 4], ctx=st2)
            qk1 = sb("qk1", [P, 2, T], F32R, st2)
            qk2 = sb("qk2", [P, 2, T], F32R, st2)
            ropea = sb("ropea", [P, T], ctx=st2)
            ropeb = sb("ropeb", [P, T], ctx=st2)
            xst2 = sb("xst2", [P, T], ctx=st2)
            V = [sb(f"V{b}", [P, QB, HEADS, 32], ctx=st2) for b in range(NB)]
            MX = sb("MX", [P, 2, 4, QB], ctx=st2)
            NM = sb("NM", [8, 2, P], F32R, st2)
            PT = sb("PT", [P, 4, T], ctx=st2)
            OT = sb("OT", [P, 2, L], ctx=st2)
            rs = sb("rs", [P, QB, 8], ctx=st2)
            ON = sb("ON", [P, QB, HEADS, HD], ctx=st2)
            OTn = sb("OTn", [P, T], ctx=st2)
            tg = sb("tg", [P, T], ctx=st2)
            sc = sb("sc", [P, NA, E], ctx=st2)
            sfc = sb("sfc", [P, NA, E], ctx=st2)
            top1 = [sb(f"top1_{n}", [P, NA, NG, GE // 2 >> n], ctx=st2) for n in range(3)]
            top2 = [sb(f"top2_{n}", [P, NA, NG, GE // 2 >> n], ctx=st2) for n in range(3)]
            low = [sb(f"low_{n}", [P, NA, NG, GE // 4 >> n], ctx=st2) for n in range(2)]
            gs = sb("gs", [P, NA, NG], ctx=st2)
            cgt = sb("cgt", [P, NA, NG, NG], ctx=st2)
            cge = sb("cge", [P, NA, NG, NG], ctx=st2)
            rank = sb("rank", [P, NA, NG], ctx=st2)
            t8 = sb("t8", [P, NA, 8], ctx=st2)
            i8 = sb("i8", [P, NA, 8], U32, ctx=st2)
            fourth = sb("fourth", [P, NA], ctx=st2)
            above = sb("above", [P, NA, E], ctx=st2)
            level = sb("level", [P, NA, E], ctx=st2)
            before4 = sb("before4", [P, NA, E], ctx=st2)
            wgt = sb("wgt", [P, NA, E], ctx=st2)
            wsum = sb("wsum", [P, NA], ctx=st2)
            pad = sb("pad", [P, 1], ctx=st2)
            w3 = sb("w3", [P, NA, 3, E], BF16, ctx=st2)
            spill = nc.dram_tensor("spill", (2, 2, P, T), F32).ap()

            def sem(name):
                return st2.enter_context(nc.semaphore(name))

            cleared = sem("cleared")
            m_tab = sem("m_tab")
            xs_done = sem("xs_done")
            rot_done = sem("rot_done")
            rot_used = sem("rot_used")
            proj_done = sem("proj_done")
            rope_done = sem("rope_done")
            first_done = sem("first_done")
            sum_done = sem("sum_done")
            second_done = sem("second_done")
            q_out = sem("q_out")
            k_out = sem("k_out")
            q_in = [sem(f"q_in{b}") for b in range(NB)]
            k_in = [sem(f"k_in{n}") for n in range(2 * NB)]
            m_in = [sem(f"m_in{u}") for u in range(UNITS)]
            qm_done = sem("qm_done")
            v_done = sem("v_done")
            v_used = sem("v_used")
            mx_done = sem("mx_done")
            mx_used = sem("mx_used")
            nmT_done = sem("nmT_done")
            nm_done = sem("nm_done")
            s_done = sem("s_done")
            p_done = sem("p_done")
            pv_done = sem("pv_done")
            ot_done = sem("ot_done")
            otT_done = sem("otT_done")
            rs_done = sem("rs_done")
            on_done = sem("on_done")
            onT_done = sem("onT_done")
            otn_done = sem("otn_done")
            g_done = sem("g_done")
            u_done = sem("u_done")
            t_done = sem("t_done")
            h1_done = sem("h1_done")
            h_done = sem("h_done")
            y_done = sem("y_done")
            yt_done = sem("yt_done")
            ytT_done = sem("ytT_done")
            res_done = sem("res_done")
            th_done = sem("th_done")
            routed = sem("routed")
            tests_done = sem("tests_done")
            picked = sem("picked")
            w3_done = sem("w3_done")
            w3t_done = sem("w3t_done")
            wT_done = sem("wT_done")

            block = st2.enter_context(nc.Block())
            MXB, SB, PVB, RA, RB = bank[0:2], bank[2:4], bank[4:6], bank[6], bank[7]
            BACK, PVLAG = 4 * LAG, 2

            @block.gpsimd
            def _(pool):
                pool.dma_start(mask[:, :], c_mask).then_inc(m_tab, 16)

                def split(i, n):
                    wait(pool, rope_done, i * 2 + (n + 1))
                    wait(pool, second_done, i * 2 + n)
                    wait(pool, (q_out, k_out)[n], i * 32)
                    pool.tensor_tensor(qk1[:, n, :], ropea[:, :], ropeb[:, :], ALU.add).then_inc(first_done, 1)
                    wait(pool, first_done, i * 2 + (n + 1))
                    pool.tensor_tensor(ropea[:, :], ropea[:, :], ropeb[:, :], ALU.add).then_inc(sum_done, 1)
                    wait(pool, sum_done, i * 2 + (n + 1))
                    pool.tensor_tensor(qk2[:, n, :], ropea[:, :], qk1[:, n, :].bitcast(F32), ALU.subtract).then_inc(second_done, 1)

                def chosen(i):
                    n = i * PICKS
                    wait(pool, tests_done, i + 1)
                    pool.tensor_tensor(level[:, :, :], level[:, :, :], before4[:, :, :], ALU.mult).then_inc(picked, 1)
                    wait(pool, picked, n + 1)
                    pool.tensor_tensor(above[:, :, :], above[:, :, :], level[:, :, :], ALU.add).then_inc(picked, 1)
                    wait(pool, picked, n + 2)
                    wait(pool, w3_done, i)
                    pool.tensor_tensor(wgt[:, :, :], above[:, :, :], sc[:, :, :], ALU.mult).then_inc(picked, 1)

                def masked(i, u):
                    b, g = u // 4, u % 4
                    if g == 0:
                        wait(pool, q_in[b], i * 48 + 48)
                    wait(pool, s_done, i * 32 - 32 + 4 * (u + 1))
                    pool.tensor_tensor(QM[0:96, u], QS[b][0:96, g, :].bitcast(F32).unsqueeze(1).broadcast_to([96, 4, L]),
                                       mask[:, :].unsqueeze(2).broadcast_to([96, 4, L]), ALU.mult).then_inc(qm_done, 1)

                def tile(i, now, before, after):
                    for u in (4, 5):
                        if now:
                            masked(i, u)
                    if after:
                        split(i + 1, 0)
                    if before:
                        chosen(i - 1)
                    if after:
                        split(i + 1, 1)
                    for u in (6, 7):
                        if now:
                            masked(i, u)
                    for u in range(4):
                        if after:
                            masked(i + 1, u)

                for n in range(2):
                    split(0, n)
                pool.wait_ge(m_tab, 16)
                for u in range(4):
                    masked(0, u)
                tiles(pool, tile)

            @block.sync
            def _(sp):
                f = lambda ap: ap.bitcast(F32)

                def spill_q(i):
                    waits(sp, (second_done, i * 2 + 1), *((s, i * 48) for s in q_in))
                    for n, part in enumerate((qk1, qk2)):
                        sp.dma_start(spill[n, 0], f(part[:, 0, :])).then_inc(q_out, 16)

                def spill_k(i):
                    waits(sp, (second_done, i * 2 + 2), *((s, i * 48) for s in k_in))
                    for n, part in enumerate((qk1, qk2)):
                        sp.dma_start(spill[n, 1], f(part[:, 1, :])).then_inc(k_out, 16)

                def load_q(i, b):
                    waits(sp, (q_out, i * 32 + 32), (qm_done, i * 8 - 8 + 4 * (b + 1)))
                    for t, part in enumerate((0, 1, 0)):
                        src = spill[part, 0, :, b * L:(b + 1) * L].rearrange("(g r) c -> r g c", g=HG)
                        sp.dma_start(f(QS[b][32 * t:32 * t + 32, :, :]), src).then_inc(q_in[b], 16)

                def load_k(i, b, half):
                    waits(sp, (k_out, i * 32 + 32), (s_done, i * 32 - 32 + 4 * (4 * b + 2 * half + 2)))
                    for t, part in enumerate((0, 0, 1)):
                        src = spill[part, 1, :, b * L:(b + 1) * L].rearrange("(g r) c -> r g c", g=HG)
                        sp.dma_start(f(KS[b][32 * t:32 * t + 32, 2 * half:2 * half + 2, :]),
                                     src[:, 2 * half:2 * half + 2, :]).then_inc(k_in[2 * b + half], 16)

                def maximum(i, u):
                    wait(sp, nm_done, i * 8 + (u + 1))
                    sp.dma_start(f(QM[LMROW:LMROW + 1, u, :, :]).rearrange("o h (q c) -> o (h q) c", q=QB),
                                 f(NM[:, u % 2, :])).then_inc(m_in[u], 16)

                def tile(i, now, before, after):
                    if before:
                        maximum(i - 1, 7)
                    if now:
                        load_k(i, 1, 0)
                        maximum(i, 0)
                        maximum(i, 1)
                        load_k(i, 1, 1)
                        maximum(i, 2)
                    if after:
                        spill_q(i + 1)
                        load_q(i + 1, 0)
                    if now:
                        maximum(i, 3)
                    if after:
                        spill_k(i + 1)
                    if now:
                        maximum(i, 4)
                    if after:
                        load_k(i + 1, 0, 0)
                    if now:
                        maximum(i, 5)
                    if after:
                        load_q(i + 1, 1)
                    if now:
                        maximum(i, 6)
                    if after:
                        load_k(i + 1, 0, 1)

                spill_q(0)
                load_q(0, 0)
                spill_k(0)
                load_k(0, 0, 0)
                load_k(0, 0, 1)
                load_q(0, 1)
                tiles(sp, tile)

            @block.tensor
            def _(pe):
                def project(i, n):
                    xr = xnT[:, bass.ds(i * T, T)]
                    pe.matmul(RB[:, :], wrot[:, n], xr, start=True, stop=True).then_inc(rot_done, 1)
                    pe.matmul(RA[:, :], wT4[:, n], xr, start=True, stop=True).then_inc(proj_done, 1)

                def project_v(i, b):
                    wait(pe, xs_done, i + 1)
                    for a in range(QB):
                        last = pe.matmul(RA[:, a * P:a * P + P], xst2[:, (QB * b + a) * P:(QB * b + a + 1) * P], wT4[:, 2],
                                         start=True, stop=True)
                    if b == NB - 1:
                        for a in range(NA):
                            last = pe.matmul(RA[:, L + a * E:L + (a + 1) * E], xst2[:, a * P:a * P + P], rwT[:, :],
                                             start=True, stop=True)
                    last.then_inc(v_done, 1)

                def maxima(i, s):
                    u, h = s // 4, s % 4
                    b, g = u // 4, u % 4
                    if h == 0:
                        wait(pe, qm_done, i * 8 + (u + 1))
                        if u % 2 == 0:
                            wait(pe, k_in[u // 2], i * 48 + 48)
                    wait(pe, mx_used, i * 32 + s - 1)
                    for q in range(QB):
                        last = pe.matmul(MXB[s % 2][:, q * L:(q + 1) * L], QM[0:96, u, h, q * P:q * P + P],
                                         KS[b][0:96, g, :], start=True, stop=True)
                    last.then_inc(mx_done, 1)

                def scores(i, s):
                    u, kb, hp = s // 4, (s // 2) % 2, s % 2
                    b, g = u // 4, u % 4
                    if s % 4 == 0:
                        wait(pe, m_in[u], i * 16 + 16)
                    wait(pe, p_done, i * 32 + s - 1)
                    pe.matmul(SB[s % 2][:, :], KS[b][0:LMROW + 1, g, kb * P:kb * P + P],
                              QM[0:LMROW + 1, u, 2 * hp:2 * hp + 2, :].rearrange("p h c -> p (h c)"),
                              start=True, stop=True).then_inc(s_done, 1)

                def values(i, s):
                    u, kb, hp = s // 4, (s // 2) % 2, s % 2
                    b, g = u // 4, u % 4
                    if s % 16 == 0:
                        wait(pe, v_used, i * 2 + (b + 1))
                    if s % 8 == 0:
                        wait(pe, ot_done, i * 4 + s // 8 - 1)
                    wait(pe, p_done, i * 32 + (s + 1))
                    for e in range(2):
                        j = 2 * hp + e
                        last = pe.matmul(PVB[g // 2][32 * j:32 * j + 32, (g % 2) * L:(g % 2 + 1) * L],
                                         V[b][:, kb, 4 * g + j, :], PT[:, s % 4, e * L:(e + 1) * L],
                                         start=(kb == 0), stop=(kb == 1))
                    last.then_inc(pv_done, 1)

                def turn_max(i, u):
                    wait(pe, mx_used, i * 32 + 4 * (u + 1))
                    wait(pe, nm_done, i * 8 + u)
                    pe.transpose(RB[0:8, 0:P], MX[:, u % 2].rearrange("p h q -> p (h q)"), ident[:, :]).then_inc(nmT_done, 1)

                def turn_out(i, k):
                    wait(pe, ot_done, i * 4 + (k + 1))
                    for q in range(QB):
                        for g in range(2):
                            last = pe.transpose(RA[:, (2 * q + g) * P:(2 * q + g + 1) * P], OT[:, g, q * P:q * P + P], ident[:, :])
                    last.then_inc(otT_done, 1)

                def turn_back(i, b):
                    wait(pe, on_done, i * 4 + 2 * (b + 1))
                    for q in range(QB):
                        last = pe.transpose(RA[:, q * P:q * P + P], ON[:, q].rearrange("p h d -> p (h d)"), ident[:, :])
                    last.then_inc(onT_done, 1)

                def gate(i):
                    pe.matmul(RA[:, :], sh[:, 0], xnT[:, bass.ds(i * T, T)], start=True, stop=True).then_inc(g_done, 1)

                def up(i):
                    pe.matmul(RB[:, :], sh[:, 1], xnT[:, bass.ds(i * T, T)], start=True, stop=True).then_inc(u_done, 1)

                def finish(i):
                    wait(pe, otn_done, i * 2 + 2)
                    wait(pe, h_done, i + 1)
                    pe.matmul(RA[:, :], wT4[:, 3], OTn[:, :], start=True, stop=False)
                    pe.matmul(RA[:, :], sh[:, 2], tg[:, :], start=False, stop=True).then_inc(y_done, 1)

                def turn_y(i):
                    wait(pe, yt_done, i + 1)
                    for a in range(NA):
                        last = pe.transpose(RB[:, a * P:a * P + P], OTn[:, a * P:a * P + P], ident[:, :])
                    last.then_inc(ytT_done, 1)

                def turn_w(i):
                    wait(pe, w3_done, i + 1)
                    for a in range(NA):
                        last = pe.transpose(RB.bitcast(BF16)[0:96, a * P:a * P + P],
                                            w3[:, a].rearrange("p k e -> p (k e)"), identb[:, :])
                    last.then_inc(w3t_done, 1)

                def tile(i, now, before, after):
                    for s in range(32):
                        if now:
                            maxima(i, s)
                        k = s - BACK
                        if (k >= 0 and now) or (k < 0 and before):
                            scores(i if k >= 0 else i - 1, k % 32)
                        k = s - BACK - PVLAG
                        if (k >= 0 and now) or (k < 0 and before):
                            values(i if k >= 0 else i - 1, k % 32)
                        if s == 0 and before:
                            wait(pe, on_done, i * 4 - 3)
                            wait(pe, yt_done, i - 1)
                            turn_out(i - 1, 1)
                        if s == 1 and before:
                            wait(pe, res_done, i - 1)
                            turn_max(i - 1, 7)
                        if s == 3 and before:
                            turn_back(i - 1, 0)
                        if s == 5 and now:
                            turn_max(i, 0)
                            wait(pe, otn_done, i * 2 - 1)
                            project_v(i, 0)
                        if s == 6 and after:
                            wait(pe, nm_done, i * 8 + 1)
                            wait(pe, v_used, i * 2 + 1)
                            project(i + 1, 0)
                        if s == 9 and now:
                            if after:
                                wait(pe, rot_used, i * 2 + 3)
                            turn_max(i, 1)
                        if s == 10 and after:
                            wait(pe, nm_done, i * 8 + 2)
                            wait(pe, rope_done, i * 2 + 3)
                            project(i + 1, 1)
                        if s == 13 and now:
                            if after:
                                wait(pe, rot_used, i * 2 + 4)
                            turn_max(i, 2)
                        if s == 13 and after:
                            wait(pe, rope_done, i * 2 + 4)
                        if s == 13 and before:
                            if now and not after:
                                wait(pe, v_used, i * 2 + 1)
                            if not now:
                                wait(pe, otn_done, i * 2 - 1)
                            turn_out(i - 1, 2)
                        if s == 15 and before:
                            wait(pe, on_done, i * 4 - 1)
                            turn_out(i - 1, 3)
                        if s == 17 and now:
                            turn_max(i, 3)
                        if s == 18 and before:
                            turn_back(i - 1, 1)
                        if s == 20 and now:
                            wait(pe, otn_done, i * 2)
                            project_v(i, 1)
                        if s == 21 and now:
                            turn_max(i, 4)
                        if s == 23 and now:
                            wait(pe, v_used, i * 2 + 2)
                            turn_out(i, 0)
                        if s == 23 and before:
                            wait(pe, nm_done, i * 8 + 5 if now else i * 8)
                            turn_w(i - 1)
                        if s == 25 and now:
                            wait(pe, wT_done, i)
                            turn_max(i, 5)
                        if s == 25 and before:
                            if now:
                                wait(pe, on_done, i * 4 + 1)
                            else:
                                wait(pe, otn_done, i * 2)
                            gate(i - 1)
                        if s == 26 and before:
                            wait(pe, wT_done, i)
                            if now:
                                wait(pe, nm_done, i * 8 + 6)
                            up(i - 1)
                        if s == 29 and now:
                            if before:
                                wait(pe, h_done, i)
                            turn_max(i, 6)
                        if s == 29 and before:
                            finish(i - 1)
                        if s == 31 and before:
                            if now:
                                wait(pe, nm_done, i * 8 + 7)
                            turn_y(i - 1)

                project(0, 0)
                pe.wait_ge(rope_done, 1)
                project(0, 1)
                pe.wait_ge(rope_done, 2)
                pe.wait_ge(cleared, 6)
                tiles(pe, tile)

            @block.scalar
            def _(act):
                act.wait_ge(cleared, 6)

                def exps(i, s):
                    wait(act, s_done, i * 32 + (s + 1))
                    wait(act, pv_done, i * 32 + s - 3)
                    act.activation(PT[:, s % 4, :], SB[s % 2][:, :], ACT.Exp,
                                   scale=1.0 / float(np.sqrt(np.float32(HD)))).then_inc(p_done, 1)

                def negmax(i, u):
                    wait(act, nmT_done, i * 8 + (u + 1))
                    if u >= 2:
                        wait(act, m_in[u - 2], i * 16 + 16)
                    else:
                        wait(act, m_in[u + 6], i * 16)
                    act.activation(NM[:, u % 2, :], RB[0:8, 0:P], ACT.Copy, scale=-1.0).then_inc(nm_done, 1)

                def outs(i, k):
                    wait(act, pv_done, i * 32 + 8 * (k + 1))
                    wait(act, otT_done, i * 4 + k)
                    act.activation(OT[:, :, :].rearrange("p g c -> p (g c)"), PVB[k % 2][:, :], ACT.Copy).then_inc(ot_done, 1)

                def outs_t(i, b):
                    wait(act, onT_done, i * 2 + (b + 1))
                    if b == 0:
                        wait(act, ytT_done, i)
                    act.activation(OTn[:, b * L:(b + 1) * L], RA[:, 0:L], ACT.Identity, bias=bcol[:, 4:5]).then_inc(otn_done, 1)

                def vals(i, b):
                    wait(act, v_done, i * 2 + (b + 1))
                    wait(act, pv_done, i * 32 - 32 + 16 * (b + 1))
                    act.activation(V[b][:, :, :, 0:HD], RA[:, 0:L].rearrange("p (a h d) -> p a h d", a=QB, h=HEADS),
                                   ACT.Copy).then_inc(v_used, 1)

                def tile(i, now, before, after):
                    for s in range(32):
                        k = s - BACK
                        if s == 2 and before:
                            negmax(i - 1, 7)
                        if s % 4 == 2 and s > 2 and now:
                            negmax(i, s // 4 - 1)
                        if s == 4 and before:
                            outs_t(i - 1, 0)
                        if s == 6 and now:
                            vals(i, 0)
                        if s == 19 and before:
                            outs_t(i - 1, 1)
                        if s == 21 and now:
                            wait(act, v_done, i * 2 + 2)
                            wait(act, picked, i * PICKS)
                            act.activation(sc[:, :, :].rearrange("p a e -> p (a e)"), RA[:, L:L + NA * E], ACT.Tanh,
                                           scale=0.5).then_inc(th_done, 1)
                            vals(i, 1)
                        if s == 24 and before:
                            wait(act, w3t_done, i)
                            act.activation(wT[:, bass.ds((i - 1) * T, T)], RB.bitcast(BF16)[0:96, 0:T], ACT.Copy).then_inc(wT_done, 1)
                        if s == 26 and before:
                            wait(act, g_done, i)
                            wait(act, y_done, i - 1)
                            act.activation(tg[:, :], RA[:, :], ACT.Tanh, scale=0.5).then_inc(t_done, 1)
                        if s == 30 and before:
                            wait(act, y_done, i)
                            wait(act, ytT_done, i - 1)
                            act.activation(OTn[:, :], RA[:, :], ACT.Identity, bias=bcol[:, 5:6]).then_inc(yt_done, 1)
                        if s in (22, 30) and now:
                            outs(i, (s - 22) // 8)
                        if s in (6, 14) and before:
                            outs(i - 1, (s + 10) // 8)
                        if (k >= 0 and now) or (k < 0 and before):
                            exps(i if k >= 0 else i - 1, k % 32)

                tiles(act, tile)

            @block.vector
            def _(v):
                v.tensor_copy(xst2[:, :], xnT[:, 0:T]).then_inc(xs_done, 1)

                def stage(i):
                    wait(v, v_done, i * 2)
                    v.tensor_copy(xst2[:, :], xnT[:, bass.ds(i * T, T)]).then_inc(xs_done, 1)

                c3 = cos[:, :].unsqueeze(1).broadcast_to([P, NB, L])
                s3 = sin[:, :].unsqueeze(1).broadcast_to([P, NB, L])
                r3 = lambda ap: ap.rearrange("p (b l) -> p b l", b=NB)

                def rope_rotated(i, n):
                    wait(v, rot_done, i * 2 + (n + 1))
                    wait(v, sum_done, i * 2 + n)
                    v.scalar_tensor_tensor(r3(ropeb[:, :]), r3(RB[:, :]), bcol[:, 2 + n:3 + n], s3, ALU.add, ALU.mult).then_inc(rot_used, 1)

                def rope_plain(i, n):
                    wait(v, proj_done, i * 2 + (n + 1))
                    wait(v, second_done, i * 2 + n)
                    v.scalar_tensor_tensor(r3(ropea[:, :]), r3(RA[:, :]), bcol[:, n:n + 1], c3, ALU.add, ALU.mult).then_inc(rope_done, 1)

                def maxima(i, s):
                    u, h = s // 4, s % 4
                    wait(v, mx_done, i * 32 + (s + 1))
                    if h == 0:
                        wait(v, nmT_done, i * 8 + u - 1)
                    v.tensor_reduce(MX[:, u % 2, h, :], MXB[s % 2][:, :].rearrange("p (q c) -> p q c", q=QB), AX.X, ALU.max).then_inc(mx_used, 1)

                def divide(i, k):
                    wait(v, otT_done, i * 4 + (k + 1))
                    o4 = RA[:, :].rearrange("p (q h c) -> p q h c", q=QB, h=8)
                    v.reciprocal(rs[:, :, :], o4[:, :, :, HD]).then_inc(rs_done, 1)
                    wait(v, rs_done, i * 4 + (k + 1))
                    if k % 2 == 0:
                        wait(v, onT_done, i * 2 + k // 2)
                    half = ON[:, :, 8 * (k % 2):8 * (k % 2) + 8, :]
                    v.tensor_tensor(half, o4[:, :, :, 0:HD], rs[:, :, :].unsqueeze(3).broadcast_to([P, QB, 8, HD]), ALU.mult).then_inc(on_done, 1)

                EARLY = {26: (0, 1, 2), 28: (3, 4), 30: (5, 6, 7)}
                LATE = {4: (8,), 5: (9,), 6: (10,), 7: (11, 12, 13), 11: (14, 15), 13: (16, 17),
                        17: (18,), 18: (19,), 19: (20, 21), 21: (22, 23, 24), 22: (25, 26)}

                def route(i, n):
                    if 0 < n <= 17:
                        v.wait_ge(routed, i * ROUTE + n)
                    elif n > 18:
                        v.wait_ge(routed, i * ROUTE + (n - 1))
                    s4 = sfc[:, :, :].rearrange("p a (g e) -> p a g e", g=NG)
                    if n == 0:
                        v.wait_ge(th_done, i + 1)
                        last = v.tensor_scalar(sc[:, :, :], sc[:, :, :], 0.5, 0.5, ALU.mult, ALU.add)
                    elif n == 1:
                        last = v.tensor_tensor(sfc[:, :, :], sc[:, :, :], rbias[:, :].unsqueeze(1).broadcast_to([P, NA, E]), ALU.add)
                    elif n == 2:
                        h = GE // 2
                        v.tensor_tensor(top1[0][:, :, :, :], s4[:, :, :, 0:h], s4[:, :, :, h:GE], ALU.max)
                        last = v.tensor_tensor(top2[0][:, :, :, :], s4[:, :, :, 0:h], s4[:, :, :, h:GE], ALU.min)
                    elif n in (3, 5):
                        m = (n - 1) // 2
                        h = GE // 2 >> m
                        t1, t2 = top1[m - 1], top2[m - 1]
                        v.tensor_tensor(top1[m][:, :, :, :], t1[:, :, :, 0:h], t1[:, :, :, h:2 * h], ALU.max)
                        v.tensor_tensor(low[m - 1][:, :, :, :], t1[:, :, :, 0:h], t1[:, :, :, h:2 * h], ALU.min)
                        last = v.tensor_tensor(top2[m][:, :, :, :], t2[:, :, :, 0:h], t2[:, :, :, h:2 * h], ALU.max)
                    elif n in (4, 6):
                        m = n // 2 - 1
                        last = v.tensor_tensor(top2[m][:, :, :, :], top2[m][:, :, :, :], low[m - 1][:, :, :, :], ALU.max)
                    elif n == 7:
                        last = v.tensor_tensor(gs[:, :, :], top1[2][:, :, :, 0], top2[2][:, :, :, 0], ALU.add)
                    elif n == 8:
                        si = gs[:, :, :].unsqueeze(3).broadcast_to([P, NA, NG, NG])
                        sj = gs[:, :, :].unsqueeze(2).broadcast_to([P, NA, NG, NG])
                        v.tensor_tensor(cgt[:, :, :, :], sj, si, ALU.is_gt)
                        last = v.tensor_tensor(cge[:, :, :, :], sj, si, ALU.is_ge)
                    elif n == 9:
                        lt = small[:, E:E + NG * NG].rearrange("p (i j) -> p i j", i=NG).unsqueeze(1).broadcast_to([P, NA, NG, NG])
                        er = small[:, E + NG * NG:E + 2 * NG * NG].rearrange("p (i j) -> p i j", i=NG).unsqueeze(1).broadcast_to([P, NA, NG, NG])
                        v.tensor_tensor(cgt[:, :, :, :], cgt[:, :, :, :], lt, ALU.mult)
                        last = v.tensor_tensor(cge[:, :, :, :], cge[:, :, :, :], er, ALU.mult)
                    elif n == 10:
                        last = v.tensor_tensor(cgt[:, :, :, :], cgt[:, :, :, :], cge[:, :, :, :], ALU.add)
                    elif n == 11:
                        last = v.tensor_reduce(rank[:, :, :], cgt[:, :, :, :], AX.X, ALU.add)
                    elif n == 12:
                        last = v.tensor_scalar(rank[:, :, :], rank[:, :, :], 2.0, None, ALU.is_lt)
                    elif n == 13:
                        last = v.tensor_tensor(s4, s4, rank[:, :, :].unsqueeze(3).broadcast_to([P, NA, NG, GE]), ALU.mult)
                    elif n == 14:
                        v.memset(pad[:, :], 0.0)
                        for a in range(NA):
                            last = v.max(t8[:, a, :], sfc[:, a, :])
                    elif n == 15:
                        wait(v, picked, i * PICKS)
                        v.tensor_tensor(above[:, :, :], sfc[:, :, :], t8[:, :, TOPK - 1:TOPK].broadcast_to([P, NA, E]), ALU.is_gt)
                        v.tensor_tensor(level[:, :, :], sfc[:, :, :], t8[:, :, TOPK - 1:TOPK].broadcast_to([P, NA, E]), ALU.is_equal)
                        for a in range(NA):
                            last = v.max_index(i8[:, a, :], t8[:, a, :], sfc[:, a, :])
                    elif n == 16:
                        last = v.tensor_copy(fourth[:, :], i8[:, :, TOPK - 1])
                    elif n == 17:
                        v.tensor_tensor(before4[:, :, :], small[:, 0:E].unsqueeze(1).broadcast_to([P, NA, E]),
                                        fourth[:, :].unsqueeze(2).broadcast_to([P, NA, E]), ALU.is_le).then_inc(tests_done, 1)
                        return
                    elif n == 18:
                        v.wait_ge(picked, i * PICKS + PICKS)
                        last = v.tensor_reduce(wsum[:, :], wgt[:, :, :], AX.X, ALU.add)
                    elif n == 19:
                        last = v.tensor_scalar(wsum[:, :], wsum[:, :], 1e-20, None, ALU.add)
                    elif n == 20:
                        last = v.reciprocal(wsum[:, :], wsum[:, :])
                    elif n == 21:
                        last = v.scalar_tensor_tensor(wgt[:, :, :], wgt[:, :, :], SCALE,
                                                      wsum[:, :].unsqueeze(2).broadcast_to([P, NA, E]), ALU.mult, ALU.mult)
                    elif n in (22, 24):
                        if n == 22:
                            wait(v, w3t_done, i)
                        last = v.tensor_copy(w3[:, :, (n - 22) // 2, :], wgt[:, :, :])
                    elif n in (23, 25):
                        last = v.tensor_tensor(wgt[:, :, :], wgt[:, :, :], w3[:, :, (n - 23) // 2, :], ALU.subtract)
                    else:
                        v.tensor_copy(w3[:, :, 2, :], wgt[:, :, :]).then_inc(w3_done, 1)
                        return
                    last.then_inc(routed, 1)

                def tile(i, now, before, after):
                    for s in range(32):
                        for n in EARLY.get(s, ()):
                            if now:
                                route(i, n)
                        for n in LATE.get(s, ()):
                            if before:
                                route(i - 1, n)
                        if s in (7, 11) and after:
                            rope_rotated(i + 1, (s - 7) // 4)
                        if s == 27 and before:
                            wait(v, t_done, i)
                            v.scalar_tensor_tensor(tg[:, :], tg[:, :], 1.0, RA[:, :], ALU.add, ALU.mult).then_inc(h1_done, 1)
                        if s in (1, 14, 16) and before:
                            divide(i - 1, {1: 1, 14: 2, 16: 3}[s])
                        if s == 24 and now:
                            divide(i, 0)
                        if now:
                            maxima(i, s)
                        if s in (7, 11) and after:
                            rope_plain(i + 1, (s - 7) // 4)
                        if s == 22 and after:
                            stage(i + 1)
                        if s == 27 and before:
                            wait(v, u_done, i)
                            wait(v, h1_done, i)
                            v.scalar_tensor_tensor(tg[:, :], tg[:, :], 0.5, RB[:, :], ALU.mult, ALU.mult).then_inc(h_done, 1)
                        if s == 31 and before:
                            wait(v, ytT_done, i)
                            k = (i - 1) * NA
                            xa = x_all[:, bass.ds(k, NA), :].rearrange("p a c -> p (a c)")
                            v.tensor_tensor(xa, RB[:, :], xa, ALU.add).then_inc(res_done, 1)

                for n in range(2):
                    rope_rotated(0, n)
                    rope_plain(0, n)
                for n in range(NB):
                    v.memset(V[n][:, :, :, :], 0.0).then_inc(cleared, 1)
                    v.memset(KS[n][LMROW:LMROW + 1, :, :].bitcast(F32), 1.0).then_inc(cleared, 1)
                v.wait_ge(cleared, 4)
                for n in range(NB):
                    v.memset(V[n][:, :, :, HD:HD + 1], 1.0).then_inc(cleared, 1)
                tiles(v, tile)

        with ExitStack() as st3:
            wgt2 = sb("wgt2", [P, 3, 2, PAIRS, 128], F32R, st3)
            xp = sb("xp", [P, 2, 2, T], F32R, st3)
            tg3 = sb("tg3", [P, 2, T], ctx=st3)
            ha = sb("ha", [P, 2, T], ctx=st3)
            hb = sb("hb", [P, 2, T], ctx=st3)
            hw = sb("hw", [P, 2, T], ctx=st3)
            h1 = sb("h1", [P, 4, T], F32R, st3)
            h2 = sb("h2", [P, 4, T], F32R, st3)
            yt3 = sb("yt3", [P, T], ctx=st3)

            def sem(name):
                return st3.enter_context(nc.semaphore(name))

            w1_done = sem("w1_done")
            w2_done = sem("w2_done")
            x1_done = sem("x1_done")
            x2_done = sem("x2_done")
            gate_done = sem("gate_done")
            up_done = sem("up_done")
            wide_done = sem("wide_done")
            t3_done = sem("t3_done")
            ha_done = sem("ha_done")
            hb_done = sem("hb_done")
            hw_done = sem("hw_done")
            h1_done = sem("h1_done")
            h2_done = sem("h2_done")
            dn_done = sem("dn_done")
            y3_done = sem("y3_done")
            y3T_done = sem("y3T_done")
            r3_done = sem("r3_done")
            stored = sem("stored")
            block = st3.enter_context(nc.Block())
            GB, UB, WB, YB, TB = bank[0:2], bank[2:4], bank[4:6], bank[6], bank[7]
            WSRC = (gT[:, :], uT[:, :], dT[:, :, :].rearrange("p n c -> p (n c)"))

            def parts(k, m):
                return wgt2[:, k, m].rearrange("p n c -> p (n c)")

            @block.tensor
            def _(pe):
                def product(out, k, p, x1, x2, start=True, stop=True):
                    pe.matmul(out, wgt2[:, k, 0, p], x1, start=start, stop=False)
                    pe.matmul(out, wgt2[:, k, 1, p], x1, start=False, stop=False)
                    return pe.matmul(out, wgt2[:, k, 0, p], x2, start=False, stop=stop)

                def up(i, p):
                    par = i % 2
                    x1, x2 = (xp[:, bass.ds(par, 1), m, :].rearrange("p o t -> p (o t)") for m in range(2))
                    if p == 0:
                        wait(pe, x2_done, i + 1)
                    n = i * PAIRS + (p - 1)
                    if p == 0 and isinstance(i, int) and i == 0:
                        pe.wait_ge(w2_done, 1)
                    wait(pe, ha_done, n)
                    product(GB[p % 2][:, :], 0, p, x1, x2).then_inc(gate_done, 1)
                    if p == 0 and isinstance(i, int) and i == 0:
                        pe.wait_ge(w2_done, 2)
                    wait(pe, hb_done, n)
                    product(UB[p % 2][:, :], 1, p, x1, x2).then_inc(up_done, 1)
                    wait(pe, hw_done, n)
                    pe.matmul(WB[p % 2][:, :], sel[:, p, :], wT[:, bass.ds(i * T, T)], start=True, stop=True).then_inc(wide_done, 1)

                def down(i, p):
                    wait(pe, h2_done, i * PAIRS + (p + 1))
                    if p == 0 and isinstance(i, int) and i == 0:
                        pe.wait_ge(w2_done, 3)
                    if p == 0:
                        wait(pe, y3_done, i)
                    product(YB[:, :], 2, p, h1[:, p % 4, :], h2[:, p % 4, :], p == 0, p == PAIRS - 1).then_inc(dn_done, 1)

                def tile(i, now, before, after):
                    for s in range(PAIRS if now else HLAG + 2):
                        p = s - HLAG
                        if now:
                            up(i, s)
                        if p < 0 and before:
                            down(i - 1, p % PAIRS)
                        if p >= 0 and now:
                            down(i, p)
                        if s == HLAG + 1 and before:
                            wait(pe, y3_done, i)
                            wait(pe, r3_done, i - 1)
                            for a in range(NA):
                                last = pe.transpose(TB[:, a * P:a * P + P], yt3[:, a * P:a * P + P], ident[:, :])
                            last.then_inc(y3T_done, 1)

                tiles(pe, tile)

            @block.scalar
            def _(act):
                def split(i):
                    wait(act, up_done, i * PAIRS - PAIRS)
                    act.activation(xp[:, bass.ds(i % 2, 1), 0, :].rearrange("p o t -> p (o t)"),
                                   xnT[:, bass.ds(i * T, T)], ACT.Copy).then_inc(x1_done, 1)

                def first(i, p):
                    wait(act, hw_done, i * PAIRS + (p + 1))
                    wait(act, dn_done, i * PAIRS + (p - 3))
                    act.activation(h1[:, p % 4, :], hw[:, p % 2, :], ACT.Copy).then_inc(h1_done, 1)

                def tile(i, now, before, after):
                    for s in range(PAIRS if now else HLAG + 1):
                        if now:
                            wait(act, gate_done, i * PAIRS + (s + 1))
                            wait(act, ha_done, i * PAIRS + (s - 1))
                            act.activation(tg3[:, s % 2, :], GB[s % 2][:, :], ACT.Tanh, scale=0.5).then_inc(t3_done, 1)
                        if s < 2 and before:
                            first(i - 1, PAIRS - 2 + s)
                        if s >= 2 and now:
                            first(i, s - 2)
                        if s == HLAG - 1 and before:
                            wait(act, dn_done, i * PAIRS)
                            wait(act, y3T_done, i - 1)
                            act.activation(yt3[:, :], YB[:, :], ACT.Copy).then_inc(y3_done, 1)
                        if s == 8 and after:
                            split(i + 1)

                split(0)
                for k, w in enumerate(WSRC):
                    act.activation(parts(k, 0), w, ACT.Copy).then_inc(w1_done, 1)

                tiles(act, tile)

            @block.gpsimd
            def _(pool):
                def split(i):
                    wait(pool, x1_done, i + 1)
                    at = bass.ds(i % 2, 1)
                    pool.tensor_tensor(xp[:, at, 1, :].rearrange("p o t -> p (o t)"), xnT[:, bass.ds(i * T, T)],
                                       xp[:, at, 0, :].rearrange("p o t -> p (o t)").bitcast(F32), ALU.subtract).then_inc(x2_done, 1)

                def second(i, p):
                    wait(pool, h1_done, i * PAIRS + (p + 1))
                    pool.tensor_tensor(h2[:, p % 4, :], hw[:, p % 2, :], h1[:, p % 4, :].bitcast(F32), ALU.subtract).then_inc(h2_done, 1)

                split(0)

                def tile(i, now, before, after):
                    for p in range(PAIRS if now else 0):
                        second(i, p)
                        if p == 8 and after:
                            split(i + 1)

                tiles(pool, tile)

            @block.vector
            def _(v):
                for k, w in enumerate(WSRC):
                    v.wait_ge(w1_done, k + 1)
                    v.tensor_tensor(parts(k, 1), w, parts(k, 0).bitcast(F32), ALU.subtract).then_inc(w2_done, 1)

                def gated(i, p):
                    k, n = p % 2, i * PAIRS + (p + 1)
                    wait(v, t3_done, n)
                    v.scalar_tensor_tensor(ha[:, k, :], tg3[:, k, :], 1.0, GB[k][:, :], ALU.add, ALU.mult).then_inc(ha_done, 1)

                def times_up(i, p):
                    k, n = p % 2, i * PAIRS + (p + 1)
                    wait(v, up_done, n)
                    wait(v, ha_done, n)
                    v.scalar_tensor_tensor(hb[:, k, :], ha[:, k, :], 0.5, UB[k][:, :], ALU.mult, ALU.mult).then_inc(hb_done, 1)

                def weighted(i, p):
                    k, n = p % 2, i * PAIRS + (p + 1)
                    wait(v, wide_done, n)
                    wait(v, hb_done, n)
                    wait(v, h2_done, n - 2)
                    v.tensor_tensor(hw[:, k, :], hb[:, k, :], WB[k][:, :], ALU.mult).then_inc(hw_done, 1)

                def tile(i, now, before, after):
                    for s in range(PAIRS if now else HLAG + 2):
                        if now:
                            gated(i, s)
                        if s > 0 and now:
                            weighted(i, s - 1)
                        if s == 0 and before:
                            weighted(i - 1, PAIRS - 1)
                        if now:
                            times_up(i, s)
                        if s == HLAG + 1 and before:
                            wait(v, y3T_done, i)
                            xa = x_all[:, bass.ds((i - 1) * NA, NA), :].rearrange("p a c -> p (a c)")
                            v.tensor_tensor(xa, TB[:, :], xa, ALU.add).then_inc(r3_done, 1)

                tiles(v, tile)

            @block.sync
            def _(sp):
                with sp.Fori(0, NT) as i:
                    sp.wait_ge(r3_done, i + 1)
                    sp.dma_start(rows(out_rows, i), x_all[:, bass.ds(i * NA, NA), :]).then_inc(stored, 16)
                sp.wait_ge(stored, 16 * NT)


_INS = ["L0_attn_x", "L0_attn_Wq", "L0_attn_bq", "L0_attn_Wk", "L0_attn_bk", "L0_attn_Wv", "L0_attn_bv",
        "L0_attn_Wo", "L0_attn_bo", "L0_ffn_router_weight", "L0_ffn_router_bias", "L0_ffn_gate_w", "L0_ffn_up_w",
        "L0_ffn_down_w", "L0_ffn_shared_gate_w", "L0_ffn_shared_up_w", "L0_ffn_shared_down_w"]


def kernel(**inputs):
    import concourse.bacc as bacc
    from concourse.bass_utils import run_bass_kernel_spmd

    nc = bacc.Bacc("TRN2", target_bir_lowering=False, num_devices=1)
    arrays = {name: np.ascontiguousarray(inputs[name]) for name in _INS}
    arrays.update(constants())
    args = [nc.dram_tensor(f"in_{name}", a.shape, mybir.dt.from_np(a.dtype), kind="ExternalInput").ap()
            for name, a in arrays.items()]
    out = nc.dram_tensor("out_y", arrays["L0_attn_x"].shape, F32, kind="ExternalOutput").ap()
    program(nc, *args, out)
    r = run_bass_kernel_spmd(nc, [{f"in_{name}": a for name, a in arrays.items()}], core_ids=[0])
    return r.results[0]["out_y"]
```
